# Optimizing a Trainium2 kernel written in Bass

```python
import numpy as np
import jax
import jax.numpy as jnp

def _softmax(x, axis=-1):
    return jax.nn.softmax(x, axis=axis)

def _gelu(x):
    return jax.nn.gelu(x, approximate=True)

def _silu(x):
    return jax.nn.silu(x)

def _sigmoid(x):
    return jax.nn.sigmoid(x)

def _layernorm(x, axis=-1, eps=1e-05):
    m = jnp.mean(x, axis=axis, keepdims=True)
    v = jnp.var(x, axis=axis, keepdims=True)
    return (x - m) / jnp.sqrt(v + eps)

def _scatter_add(tgt, idx, src, axis=0):
    return tgt.at[idx].add(src)

def _segment_sum(src, seg, n):
    return jax.ops.segment_sum(src, seg, n)
kernel_name = 'mk_seq_preln_d1_jaxref_r8_c4ad2c'

def setup_inputs(seed: int=0):
    np.random.seed(seed)
    _w = jnp.asarray

    def _L0_attn_setup():
        import jax, jax.numpy as jnp
        import numpy as np
        B, S, D = (4, 256, 128)
        H, K = (16, 64)
        EPS = 0.001
        key = jax.random.key(seed)
        ks = jax.random.split(key, 11)
        s = 0.02
        return {'x': jax.random.normal(ks[0], (B, S, D), jnp.float32), 'Wq': jax.random.normal(ks[1], (D, H, K), jnp.float32) * s, 'bq': jnp.zeros((H, K), jnp.float32), 'Wk': jax.random.normal(ks[2], (D, H, K), jnp.float32) * s, 'bk': jnp.zeros((H, K), jnp.float32), 'Wv': jax.random.normal(ks[3], (D, H, K), jnp.float32) * s, 'bv': jnp.zeros((H, K), jnp.float32), 'Wo': jax.random.normal(ks[4], (H, K, D), jnp.float32) * s, 'bo': jnp.zeros((D,), jnp.float32), 'gamma': jnp.ones((D,), jnp.float32), 'beta': jnp.zeros((D,), jnp.float32)}
    _L0_attn_in = _L0_attn_setup()

    def _L0_ffn_setup():
        import jax, jax.numpy as jnp
        import numpy as np
        H = 128
        I = 64
        E = 64
        G = 8
        TOPK_GROUP = 4
        K = 8
        I_SH = 128
        SCALE = 2.5

        def _route(x, router_w, e_bias):
            T = x.shape[0]
            scores = jax.nn.sigmoid(x.astype(jnp.float32) @ router_w.T.astype(jnp.float32))
            sfc = jax.lax.stop_gradient(scores) + e_bias[None, :]
            group_scores = jax.lax.top_k(sfc.reshape(T, G, E // G), 2)[0].sum(-1)
            _, gidx = jax.lax.top_k(group_scores, TOPK_GROUP)
            gmask = jax.nn.one_hot(gidx, G, dtype=sfc.dtype).sum(1)
            smask = jnp.repeat(gmask, E // G, axis=1)
            masked = jnp.where(smask > 0, sfc, 0.0)
            _, topk_idx = jax.lax.top_k(masked, K)
            w = jnp.take_along_axis(scores, topk_idx, axis=1)
            w = w / (w.sum(-1, keepdims=True) + 1e-20)
            return (topk_idx, w * SCALE)
        key = jax.random.key(seed)
        ks = jax.random.split(key, 9)
        s = 0.02
        return {'hidden_states': jax.random.normal(ks[0], (2, 128, H), jnp.float32), 'router_w': jax.random.normal(ks[1], (E, H), jnp.float32) * s, 'e_bias': jnp.zeros((E,), jnp.float32), 'Wg': jax.random.normal(ks[2], (E, H, I), jnp.float32) * s, 'Wu': jax.random.normal(ks[3], (E, H, I), jnp.float32) * s, 'Wd': jax.random.normal(ks[4], (E, I, H), jnp.float32) * s, 'SWg': jax.random.normal(ks[5], (H, I_SH), jnp.float32) * s, 'SWu': jax.random.normal(ks[6], (H, I_SH), jnp.float32) * s, 'SWd': jax.random.normal(ks[7], (I_SH, H), jnp.float32) * s}
    _L0_ffn_in = _L0_ffn_setup()
    _d = {'L0_attn_x': _L0_attn_in['x'], 'L0_attn_Wq': _L0_attn_in['Wq'], 'L0_attn_bq': _L0_attn_in['bq'], 'L0_attn_Wk': _L0_attn_in['Wk'], 'L0_attn_bk': _L0_attn_in['bk'], 'L0_attn_Wv': _L0_attn_in['Wv'], 'L0_attn_bv': _L0_attn_in['bv'], 'L0_attn_Wo': _L0_attn_in['Wo'], 'L0_attn_bo': _L0_attn_in['bo'], 'L0_attn_gamma': _L0_attn_in['gamma'], 'L0_attn_beta': _L0_attn_in['beta'], 'L0_ffn_router_w': _L0_ffn_in['router_w'], 'L0_ffn_e_bias': _L0_ffn_in['e_bias'], 'L0_ffn_Wg': _L0_ffn_in['Wg'], 'L0_ffn_Wu': _L0_ffn_in['Wu'], 'L0_ffn_Wd': _L0_ffn_in['Wd'], 'L0_ffn_SWg': _L0_ffn_in['SWg'], 'L0_ffn_SWu': _L0_ffn_in['SWu'], 'L0_ffn_SWd': _L0_ffn_in['SWd']}
    _x0 = _d['L0_attn_x']
    _d['L0_attn_x'] = jax.random.normal(jax.random.fold_in(jax.random.key(seed), 1), (8, 512, 128), dtype=_x0.dtype)
    del _x0
    return _d

def reference(L0_attn_x, L0_attn_Wq, L0_attn_bq, L0_attn_Wk, L0_attn_bk, L0_attn_Wv, L0_attn_bv, L0_attn_Wo, L0_attn_bo, L0_attn_gamma, L0_attn_beta, L0_ffn_router_w, L0_ffn_e_bias, L0_ffn_Wg, L0_ffn_Wu, L0_ffn_Wd, L0_ffn_SWg, L0_ffn_SWu, L0_ffn_SWd):

    def _L0_attn_ref(x, Wq, bq, Wk, bk, Wv, bv, Wo, bo, gamma, beta):
        import jax, jax.numpy as jnp
        import numpy as np
        B, S, D = (4, 256, 128)
        H, K = (16, 64)
        EPS = 0.001
        q = jnp.einsum('bsd,dhk->bshk', x, Wq) + bq
        k = jnp.einsum('bsd,dhk->bshk', x, Wk) + bk
        v = jnp.einsum('bsd,dhk->bshk', x, Wv) + bv
        scale = 1.0 / jnp.sqrt(jnp.asarray(K, x.dtype))
        scores = jnp.einsum('bqhk,bshk->bhqs', q, k) * scale
        attn = jax.nn.softmax(scores, axis=-1)
        ctx = jnp.einsum('bhqs,bshk->bqhk', attn, v)
        attn_out = jnp.einsum('bqhk,hkd->bqd', ctx, Wo) + bo
        y = x + attn_out
        mu = jnp.mean(y, axis=-1, keepdims=True)
        var = jnp.mean(jnp.square(y - mu), axis=-1, keepdims=True)
        return (y - mu) * jax.lax.rsqrt(var + EPS) * gamma + beta

    def _L0_ffn_ref(hidden_states, router_w, e_bias, Wg, Wu, Wd, SWg, SWu, SWd):
        import jax, jax.numpy as jnp
        import numpy as np
        H = 128
        I = 64
        E = 64
        G = 8
        TOPK_GROUP = 4
        K = 8
        I_SH = 128
        SCALE = 2.5

        def _route(x, router_w, e_bias):
            T = x.shape[0]
            scores = jax.nn.sigmoid(x.astype(jnp.float32) @ router_w.T.astype(jnp.float32))
            sfc = jax.lax.stop_gradient(scores) + e_bias[None, :]
            group_scores = jax.lax.top_k(sfc.reshape(T, G, E // G), 2)[0].sum(-1)
            _, gidx = jax.lax.top_k(group_scores, TOPK_GROUP)
            gmask = jax.nn.one_hot(gidx, G, dtype=sfc.dtype).sum(1)
            smask = jnp.repeat(gmask, E // G, axis=1)
            masked = jnp.where(smask > 0, sfc, 0.0)
            _, topk_idx = jax.lax.top_k(masked, K)
            w = jnp.take_along_axis(scores, topk_idx, axis=1)
            w = w / (w.sum(-1, keepdims=True) + 1e-20)
            return (topk_idx, w * SCALE)
        orig_shape = hidden_states.shape
        x = hidden_states.reshape(-1, orig_shape[-1])
        T = x.shape[0]
        topk_idx, topk_w = _route(x, router_w, e_bias)
        coef = jnp.zeros((T, E), topk_w.dtype).at[jnp.arange(T)[:, None], topk_idx].add(topk_w)
        g = jnp.einsum('th,ehi->tei', x, Wg)
        u = jnp.einsum('th,ehi->tei', x, Wu)
        h = jax.nn.silu(g) * u * coef[:, :, None]
        moe_out = jnp.einsum('tei,eih->th', h, Wd)
        shared = jax.nn.silu(x @ SWg) * (x @ SWu) @ SWd
        return (moe_out + shared).reshape(orig_shape)
    x = L0_attn_x
    x = x + _L0_attn_ref(_layernorm(x, axis=-1), L0_attn_Wq, L0_attn_bq, L0_attn_Wk, L0_attn_bk, L0_attn_Wv, L0_attn_bv, L0_attn_Wo, L0_attn_bo, L0_attn_gamma, L0_attn_beta)
    x = x + _L0_ffn_ref(_layernorm(x, axis=-1), L0_ffn_router_w, L0_ffn_e_bias, L0_ffn_Wg, L0_ffn_Wu, L0_ffn_Wd, L0_ffn_SWg, L0_ffn_SWu, L0_ffn_SWd)
    return x

_drawn_inputs = setup_inputs


def setup_inputs(seed=0):
    import zlib

    import numpy as np

    out = dict(_drawn_inputs(seed))
    spreads = {'L0_attn_bq': (0.0, 0.8),
     'L0_attn_bk': (0.0, 0.8),
     'L0_attn_bv': (0.0, 0.1),
     'L0_attn_bo': (0.0, 0.1),
     'L0_attn_gamma': (1.0, 0.2),
     'L0_attn_beta': (0.0, 0.1),
     'L0_ffn_e_bias': (0.0, 0.8)}
    factors = {'L0_attn_Wq': 8.0,
     'L0_attn_Wk': 8.0,
     'L0_attn_Wv': 8.0,
     'L0_ffn_router_w': 8.0,
     'L0_ffn_Wg': 8.0,
     'L0_ffn_Wu': 8.0,
     'L0_ffn_Wd': 8.0,
     'L0_ffn_SWg': 8.0,
     'L0_ffn_SWu': 8.0,
     'L0_ffn_SWd': 8.0}
    for name, (base, spread) in spreads.items():
        noise = np.random.default_rng([zlib.crc32(name.encode()), seed]).standard_normal(out[name].shape)
        drawn = base * np.exp(spread * noise) if base else spread * noise
        out[name] = jnp.asarray(drawn.astype(out[name].dtype))
    for name, factor in factors.items():
        out[name] = (out[name] * factor).astype(out[name].dtype)
    return out
```

```python
from contextlib import ExitStack

import concourse.bass as bass
from concourse import mybir

P = 128
F32 = mybir.dt.float32
F16 = mybir.dt.float16
BF16 = mybir.dt.bfloat16
ALU = mybir.AluOpType
ACT = mybir.ActivationFunctionType
AX = mybir.AxisListType

B, S, D = 8, 512, 128
H, K = 16, 64
HP = H // 2
PAIRS = B * HP
QT = S // P
TOK = B * S
NT = TOK // P
E, G, TOPG, TOPK = 64, 8, 4, 8
EG = E // G
EP = E // 2
TILES = EP + 1
ROUTE_SCALE = 2.5
LN_EPS, POST_EPS = 1e-5, 1e-3
ROW_SCALE = 1024.0
EXP_SHIFT = 5.0
Q1, Q2, K1, K2 = range(4)
ZQH, ZQL, ZKH, ZKL = range(4)
UNROLL = HP
FIRST, LAST = 4, 60


def layer(nc, x, Wq, bq, Wk, bk, Wv, bv, Wo, bo, gamma, beta, router_w, e_bias,
          Wg, Wu, Wd, SWg, SWu, SWd, out):
    with ExitStack() as ctx:
        def sem(name):
            return ctx.enter_context(nc.semaphore(name))

        ARENA = 53100
        arena = ctx.enter_context(nc.sbuf_tensor("arena", [P, ARENA], F32))
        top = [0]

        def take(words, at=None):
            if at is None:
                at = top[0]
                top[0] += words
                assert top[0] <= ARENA, top[0]
            return arena[:, at:at + words]

        def f16(ap):
            return ap.bitcast(F16)

        xn = take(NT * D).rearrange("p (t d) -> p t d", t=NT)
        xT_hi = f16(take(TOK // 2))
        xT_lo = f16(take(TOK // 2))
        ident = take(P)
        ident16 = f16(take(P // 2))
        gamma_b, beta_b, attn_bias = take(D), take(D), take(D)
        ebias_b = take(E)
        router_hi, router_lo = f16(take(E // 2)), f16(take(E // 2))
        bq8, bk_c, bv_c = take(HP), take(HP), take(HP)
        stat = take(8 * NT).rearrange("p (k t) -> p k t", k=8)
        tri = take(G * G)
        gate_hi, gate_lo, up_hi, up_lo, down_hi, down_lo = (
            f16(take(TILES * P // 2)).rearrange("p (t n) -> p t n", t=TILES) for _ in range(6))
        base = top[0]
        wqkv_at = top[0]
        wq_hi, wq_lo, wk_hi, wk_lo, wv_hi, wv_lo = (
            f16(take(H * K // 2)).rearrange("p (n c) -> p n c", n=HP) for _ in range(6))
        wo_hi, wo_lo = (f16(take(HP * D // 2)).rearrange("p (n c) -> p n c", n=HP) for _ in range(2))
        stack_at = top[0]
        stack = f16(take(4 * 2 * 4 * S // 2)).rearrange("p (r h k q) -> p r h k q", r=4, h=2, k=4)
        flat = f16(take(2 * 4 * S // 2)).rearrange("p (r k q) -> p r k q", r=2, k=4)
        v_hi = f16(take(2 * QT * 2 * (K + 1) // 2)).rearrange("p (r t h c) -> p r t h c", r=2, t=QT, h=2)
        v_lo = f16(take(2 * QT * 2 * K // 2)).rearrange("p (r t h c) -> p r t h c", r=2, t=QT, h=2)
        num_at = top[0]
        num_flat = take(2 * QT * 2 * S)
        num = num_flat.rearrange("p (r t h q) -> p r t h q", r=2, t=QT, h=2)
        num_hi = num_flat.bitcast(BF16).rearrange("p (r t h q w) -> p r t h q w", r=2, t=QT, h=2, w=2)
        numlo_at = top[0]
        num_lo = f16(take(2 * QT * 2 * S // 2)).rearrange("p (r t h q) -> p r t h q", r=2, t=QT, h=2)
        ctxn = take(2 * QT * P).rearrange("p (r t c) -> p r t c", r=2, t=QT)
        ctxT_hi = f16(take(2 * S // 2)).rearrange("p (r q) -> p r q", r=2)
        ctxT_lo = f16(take(2 * S // 2)).rearrange("p (r q) -> p r q", r=2)
        rmax = take(2 * QT * 2).rearrange("p (r t h) -> p r t h", r=2, t=QT)
        negmax = f16(take(2 * QT)).rearrange("p (r t h) -> p r t h", r=2, t=QT)
        rden = take(2 * 2).rearrange("p (r t) -> p r t", r=2)
        raw_q, raw_k, raw_v, raw_o = (take(H * K, num_at + i * H * K) for i in range(4))
        bv_rows = take(HP * P, num_at + 4 * H * K).rearrange("p (n c) -> p n c", n=HP)
        router_raw = take(D, num_at + 5 * H * K)
        bo_b = take(D, num_at + 5 * H * K + D)
        ones = take(S, num_at + 5 * H * K + 2 * D)
        raw_at = stack_at
        raw_g, raw_u, raw_d = (take(TILES * P, raw_at + i * TILES * P).rearrange("p (t n) -> p t n", t=TILES)
                               for i in range(3))
        c_at = raw_at + 3 * TILES * P
        x_again = take(NT * D, c_at).rearrange("p (t d) -> p t d", t=NT)
        xf = x_again
        r_at = c_at + NT * D
        coefT = f16(take(TOK // 2, r_at + 2 * NT * E))
        scores = take(NT * E, r_at).rearrange("p (t e) -> p t e", t=NT)
        sfc = take(NT * E, r_at + NT * E).rearrange("p (t e) -> p t e", t=NT)
        work1 = take(NT * E, wqkv_at)
        work2 = take(NT * E, wqkv_at + NT * E)
        work3 = take(NT * E, c_at)
        work4 = take(NT * E, c_at + NT * E)
        d_at = stack_at
        sel = f16(take(EP * P // 2, d_at)).rearrange("p (j h m) -> p j h m", j=EP, h=2)
        d_at += EP * P // 2
        silu_g = take(2 * S, d_at).rearrange("p (r q) -> p r q", r=2)
        prod = take(2 * S, d_at + 2 * S).rearrange("p (r q) -> p r q", r=2)
        hid = take(3 * S, d_at + 4 * S).rearrange("p (r q) -> p r q", r=3)
        hid_hi = f16(take(3 * S // 2, d_at + 7 * S)).rearrange("p (r q) -> p r q", r=3)
        hid_lo = f16(take(3 * S // 2, d_at + 7 * S + 3 * S // 2)).rearrange("p (r q) -> p r q", r=3)
        ysb = take(S, d_at + 10 * S)

        bank = [ctx.enter_context(nc.psum_tensor(f"bank{i}", [P, 1024], F32)) for i in range(4)]
        ps_st = [bank[0], bank[1]]
        ps8 = [bank[i // 2][:, (i % 2) * 512:(i % 2) * 512 + 512] for i in range(8)]
        ps_max = ps8[4]
        ps_ctx = ps8[5]
        ps_proj = ps8[6]
        ps_turn = ps8[7]

        in_x = sem("in_x")
        in_w = sem("in_w")
        in_small = sem("in_small")
        in_again = sem("in_again")
        in_ffn = sem("in_ffn")
        dve_step = sem("dve_step")
        act_step = sem("act_step")
        pool_const = sem("pool_const")
        tr_a = sem("tr_a")
        tr_a_hi = sem("tr_a_hi")
        tr_a_lo = sem("tr_a_lo")
        bias_done = sem("bias_done")
        router_t = sem("router_t")
        a_rstd = sem("a_rstd")
        qk_proj = sem("qk_proj")
        qk_hi = sem("qk_hi")
        qk_lo = sem("qk_lo")
        v_proj = sem("v_proj")
        v_hi_done = sem("v_hi_done")
        v_lo_done = sem("v_lo_done")
        stacked = [sem("stacked0"), sem("stacked1")]
        max_scores = sem("max_scores")
        max_done = sem("max_done")
        negmax_done = sem("negmax_done")
        maxrow_ps = sem("maxrow_ps")
        maxrow = sem("maxrow")
        scores_t = sem("scores_t")
        exp_done = sem("exp_done")
        lo_pool = sem("lo_pool")
        lo_dve = sem("lo_dve")
        ctx_ps = sem("ctx_ps")
        rden_done = sem("rden_done")
        ctx_done = sem("ctx_done")
        ctx_t = sem("ctx_t")
        ctx_hi = sem("ctx_hi")
        ctx_lo = sem("ctx_lo")
        y_ps = sem("y_ps")
        y_added = sem("y_added")
        tr_c = sem("tr_c")
        tr_c_hi = sem("tr_c_hi")
        tr_c_lo = sem("tr_c_lo")
        logits = sem("logits")
        sigm = sem("sigm")
        coef_t = sem("coef_t")
        coef_sb = sem("coef_sb")
        ffn_w_hi = sem("ffn_w_hi")
        ffn_w_lo = sem("ffn_w_lo")
        sel_done = sem("sel_done")
        g_ps = sem("g_ps")
        uc_ps = sem("uc_ps")
        silu_done = sem("silu_done")
        prod_done = sem("prod_done")
        hid_done = sem("hid_done")
        hid_hi_done = sem("hid_hi_done")
        hid_lo_done = sem("hid_lo_done")
        down_done = sem("down_done")
        y_copied = sem("y_copied")
        y_back = sem("y_back")
        out_ready = sem("out_ready")
        out_sent = sem("out_sent")

        def wait(eng, s, value):
            if isinstance(value, int) and value <= 0:
                return
            eng.wait_ge(s, value)

        def upto(value, most):
            return min(value, most) if isinstance(value, int) else value

        def valid(pair, off=0):
            return not isinstance(pair, int) or 0 <= pair + off < PAIRS

        def steps(run, eng):
            for p in range(-3, FIRST):
                run(p, p % UNROLL, p // HP)
            with eng.Fori(0, (LAST - FIRST) // UNROLL) as i:
                for u in range(UNROLL):
                    run(i * UNROLL + (FIRST + u), (FIRST + u) % UNROLL, i + (FIRST + u) // HP)
            for p in range(LAST, PAIRS + 3):
                run(p, p % UNROLL, p // HP)

        def batch_of(u, batch, off):
            return (u + off) % HP, batch + (u + off) // HP

        block = ctx.enter_context(nc.Block())

        @block.sync
        def _(sp):
            xv = x.rearrange("b (t p) d -> p (b t) d", p=P)
            for c in range(4):
                n = NT // 4
                sp.dma_start(xn[:, c * n:(c + 1) * n, :], xv[:, c * n:(c + 1) * n, :]).then_inc(in_x, 16)
            sp.dma_start(raw_q, Wq.rearrange("d h k -> d (h k)")).then_inc(in_w, 16)
            sp.dma_start(raw_k, Wk.rearrange("d h k -> d (h k)")).then_inc(in_w, 16)
            sp.dma_start(raw_v, Wv.rearrange("d h k -> d (h k)")).then_inc(in_w, 16)
            sp.dma_start(raw_o.rearrange("p (n c) -> p n c", n=HP),
                         Wo.rearrange("h k d -> (h k) d").rearrange("(n p) d -> p n d", p=P)).then_inc(in_w, 16)
            with nc.allow_non_contiguous_dma(reason="small vectors"):
                for dst, src in ((bq8, bq), (bk_c, bk), (bv_c, bv)):
                    sp.dma_start(dst, src.rearrange("h k -> (h k)").rearrange("(n p) -> p n", p=P)).then_inc(in_small, 16)
                for dst, src in ((gamma_b, gamma), (beta_b, beta), (bo_b, bo), (ebias_b, e_bias)):
                    sp.dma_start(dst, src.partition_broadcast(P)).then_inc(in_small, 16)
            sp.dma_start(router_raw[0:E, :], router_w).then_inc(in_small, 16)

            def run(p, u, batch):
                t = p + 3
                if valid(t):
                    wait(sp, scores_t, 4 * p)
                    r, z, odd = (u + 3) % 4, (u + 3) % 2, (u + 3) % 2
                    sp.wait_ge(qk_lo, 2 * t + 2)
                    for h in range(2):
                        a = flat[h * K:(h + 1) * K, z, :, :]
                        high, low = stack[0:K, r, h, :, :], stack[K:P, r, h, :, :]
                        sp.dma_start(high[:, Q1:Q2 + 1, :], a[:, ZQH:ZQH + 1, :].broadcast_to([K, 2, S])).then_inc(stacked[odd], 16)
                        sp.dma_start(high[:, K1:K2 + 1, :], a[:, ZKH:ZKL + 1, :]).then_inc(stacked[odd], 16)
                        sp.dma_start(low[:, Q1:K1 + 1:2, :], a[:, ZQL:ZKH + 1, :]).then_inc(stacked[odd], 16)

            steps(run, sp)

            sp.wait_ge(y_added, PAIRS)
            sp.dma_start(x_again, xv).then_inc(in_again, 16)
            sp.dma_start(raw_g[:, 0, :], SWg).then_inc(in_ffn, 16)
            sp.dma_start(raw_u[:, 0, :], SWu).then_inc(in_ffn, 16)
            sp.dma_start(raw_d[:, 0, :], SWd).then_inc(in_ffn, 16)
            sp.dma_start(raw_g[:, 1:, :].rearrange("p t (e i) -> p (t e) i", e=2), Wg.rearrange("e h i -> h e i")).then_inc(in_ffn, 16)
            sp.dma_start(raw_u[:, 1:, :].rearrange("p t (e i) -> p (t e) i", e=2), Wu.rearrange("e h i -> h e i")).then_inc(in_ffn, 16)
            sp.dma_start(raw_d[:, 1:, :], Wd.rearrange("e i h -> (e i) h").rearrange("(t p) h -> p t h", p=P)).then_inc(in_ffn, 16)

            ov = out.rearrange("b (t p) d -> b p t d", p=P)
            for n in range(B):
                sp.wait_ge(out_ready, n + 1)
                sp.dma_start(ov[n], xn[:, n * QT:(n + 1) * QT, :]).then_inc(out_sent, 16)
            sp.wait_ge(out_sent, 16 * B)

        @block.gpsimd
        def _(pool):
            pool.memset(ident, 0.0).then_inc(pool_const, 1)
            pool.wait_ge(pool_const, 1)
            pool.affine_select(out=ident, in_=ident, compare_op=ALU.not_equal, fill=1.0, base=0,
                               pattern=[[-1, P]], channel_multiplier=1).then_inc(pool_const, 1)
            pool.memset(tri, 1.0).then_inc(pool_const, 1)
            pool.wait_ge(pool_const, 3)
            pool.affine_select(out=tri.rearrange("p (g h) -> p g h", g=G), in_=tri.rearrange("p (g h) -> p g h", g=G),
                               compare_op=ALU.is_gt, fill=0.0, base=0, pattern=[[1, G], [-1, G]],
                               channel_multiplier=0).then_inc(pool_const, 1)
            pool.memset(ones, 1.0).then_inc(pool_const, 1)
            pool.memset(v_hi[:, :, :, :, K:K + 1], 1.0).then_inc(pool_const, 1)
            pool.wait_ge(pool_const, 6)

            def run(p, u, batch):
                def lo(s):
                    pool.wait_ge(exp_done, 4 * p + s + 1)
                    if s == 0:
                        wait(pool, ctx_ps, 4 * (p - 2) + 4)
                    pool.tensor_tensor(num_lo[:, u % 2, s, :, :], num[:, u % 2, s, :, :],
                                       num_hi[:, u % 2, s, :, :, 1], ALU.subtract).then_inc(lo_pool, 1)

                if valid(p):
                    for s in (0, 2, 3):
                        lo(s)

            steps(run, pool)

            pool.wait_ge(ffn_w_lo, 6)
            pool.memset(sel, 0.0).then_inc(sel_done, 1)
            pool.wait_ge(sel_done, 1)
            for n, off in enumerate((0, E)):
                pool.affine_select(out=sel, in_=sel, compare_op=ALU.not_equal, fill=1.0, base=-off,
                                   pattern=[[-2, EP], [-1, 2], [0, E]], channel_multiplier=1).then_inc(sel_done, 1)
                pool.wait_ge(sel_done, 2 + n)

            def tile(t, r):
                pool.wait_ge(hid_hi_done, t + 1)
                wait(pool, down_done, t - 2)
                pool.tensor_tensor(hid_lo[:, r % 3, :], hid[:, r % 3, :], hid_hi[:, r % 3, :],
                                   ALU.subtract).then_inc(hid_lo_done, 1)

            for t in range(6):
                tile(t, t)
            with pool.Fori(1, TILES * B // 6) as i:
                for r in range(6):
                    tile(i * 6 + r, r)

        @block.scalar
        def _(act):
            n_act = [0]

            def step(ins):
                ins.then_inc(act_step, 1)
                n_act[0] += 1

            act.wait_ge(dve_step, A_VAR)
            nc.scalar.activation(stat[:, 7, :], stat[:, 6, :], ACT.Sqrt).then_inc(a_rstd, 1)
            act.wait_ge(in_w, 64)
            act.wait_ge(in_small, 8 * 16)
            step(nc.scalar.activation(wq_hi, raw_q.rearrange("p (n c) -> p n c", n=HP), ACT.Copy, scale=K ** -0.5))
            step(nc.scalar.activation(wk_hi, raw_k.rearrange("p (n c) -> p n c", n=HP), ACT.Copy))
            step(nc.scalar.activation(wv_hi, raw_v.rearrange("p (n c) -> p n c", n=HP), ACT.Copy))
            step(nc.scalar.activation(wo_hi, raw_o.rearrange("p (n c) -> p n c", n=HP), ACT.Copy))
            act.wait_ge(pool_const, 2)
            step(nc.scalar.activation(ident16, ident, ACT.Copy))
            act.wait_ge(router_t, 1)
            step(nc.scalar.activation(router_hi, ps8[6][:, 0:E], ACT.Copy))

            def hi_block(n, ready, done):
                act.wait_ge(ready, n + 1)
                nc.scalar.activation(xT_hi[:, n * S:(n + 1) * S], ps8[n % 4], ACT.Copy).then_inc(done, 1)

            for n in range(B):
                hi_block(n, tr_a, tr_a_hi)

            def run(p, u, batch):
                t = p + 3

                def hi(which, n):
                    act.wait_ge(qk_proj, 2 * t + which + 1)
                    if which == 0 and (not isinstance(t, int) or t >= 2):
                        act.wait_ge(max_scores, 8 * (t - 2) + 1)
                    bias = (bq8, bk_c)[which]
                    nc.scalar.activation(flat[:, (u + 3) % 2, (ZQH, ZKH)[which], :], ps_proj, ACT.Identity,
                                         bias=bias[:, n:n + 1]).then_inc(qk_hi, 1)

                for s in range(4):
                    if valid(p):
                        act.wait_ge(scores_t, 4 * p + s + 1)
                        if s == 0:
                            wait(act, ctx_ps, 4 * (p - 2) + 4)
                        nc.scalar.activation(num[:, u % 2, s, :, :],
                                             ps_st[s % 2][:, :].rearrange("p (h q) -> p h q", h=2),
                                             ACT.Exp).then_inc(exp_done, 1)
                    if s == 2 and valid(p, 1):
                        act.wait_ge(maxrow_ps, p + 1 + 1)
                        nc.scalar.activation(stack[K:K + 2, (u + 1) % 4, :, Q2, :],
                                             ps_turn[K:K + 2, :].unsqueeze(1).broadcast_to([2, 2, S]),
                                             ACT.Copy).then_inc(maxrow, 1)
                    if valid(p, -1):
                        h, q0 = s // 2, 2 * (s % 2)
                        act.wait_ge(rden_done, 4 * (p - 1) + s + 1)
                        if s == 0:
                            wait(act, ctx_t, p - 3 + 1)
                        for q in range(2):
                            last = nc.scalar.activation(ctxn[:, (u + 1) % 2, q0 + q, h * K:(h + 1) * K],
                                                        ps_ctx[:, q * P:q * P + K], ACT.Copy,
                                                        scale=rden[:, s % 2, q:q + 1])
                        last.then_inc(ctx_done, 1)
                    if s == 0 and valid(t):
                        hi(0, batch_of(u, batch, 3)[0])
                    if s == 1 and valid(t):
                        hi(1, batch_of(u, batch, 3)[0])
                    if s == 2 and valid(p):
                        act.wait_ge(v_proj, p + 1)
                        wait(act, ctx_ps, 4 * (p - 2) + 4)
                        nc.scalar.activation(v_hi[:, u % 2, :, :, 0:K],
                                             ps_proj.rearrange("p (t h c) -> p t h c", t=QT, h=2),
                                             ACT.Copy).then_inc(v_hi_done, 1)
                    if s == 0 and valid(p, -2):
                        act.wait_ge(ctx_t, p - 2 + 1)
                        wait(act, y_ps, p - 4 + 1)
                        nc.scalar.activation(ctxT_hi[:, u % 2, :], ps_turn, ACT.Copy).then_inc(ctx_hi, 1)

            steps(run, act)

            act.wait_ge(in_ffn, 6 * 16)
            act.wait_ge(dve_step, C_VAR1)
            nc.scalar.activation(stat[:, 7, :], stat[:, 6, :], ACT.Sqrt).then_inc(a_rstd, 1)
            for dst, src in ((gate_hi, raw_g), (up_hi, raw_u), (down_hi, raw_d)):
                nc.scalar.activation(dst, src, ACT.Copy).then_inc(ffn_w_hi, 1)
            act.wait_ge(dve_step, C_VAR2)
            nc.scalar.activation(stat[:, 7, :], stat[:, 6, :], ACT.Sqrt).then_inc(a_rstd, 1)
            for n in range(B):
                hi_block(n, tr_c, tr_c_hi)
            for n in range(NT * E // 512):
                act.wait_ge(logits, n + 1)
                nc.scalar.activation(scores[:, 8 * n:8 * n + 8, :], ps8[4 + n].rearrange("p (t e) -> p t e", t=8),
                                     ACT.Sigmoid).then_inc(sigm, 1)
            for n in range(NT // 4):
                act.wait_ge(coef_t, n + 1)
                nc.scalar.activation(coefT[:, n * S:(n + 1) * S], ps8[n % 4].bitcast(F16)[:, 0:S],
                                     ACT.Copy).then_inc(coef_sb, 1)

            def silu(t, r):
                act.wait_ge(g_ps, t + 1)
                wait(act, prod_done, t - 1)
                nc.scalar.activation(silu_g[:, r % 2, :], ps8[r % 2], ACT.Silu).then_inc(silu_done, 1)

            def hid_hi_tile(t, r):
                act.wait_ge(hid_done, t + 1)
                wait(act, down_done, t - 2)
                nc.scalar.activation(hid_hi[:, r % 3, :], hid[:, r % 3, :], ACT.Copy).then_inc(hid_hi_done, 1)

            last = TILES * B - 1
            silu(0, 0)
            for t in range(5):
                silu(t + 1, t + 1)
                hid_hi_tile(t, t)
            with act.Fori(1, TILES * B // 6) as i:
                for r in range(6):
                    silu(i * 6 + r, r)
                    hid_hi_tile(i * 6 + (r - 1), (r - 1) % 6)
            hid_hi_tile(last, last % 6)

        @block.vector
        def _(dve):
            n_step = [0]

            def step(ins):
                ins.then_inc(dve_step, 1)
                n_step[0] += 1
                dve.wait_ge(dve_step, n_step[0])

            def step_no_wait(ins):
                ins.then_inc(dve_step, 1)
                n_step[0] += 1

            def variance(src, stats, eps, expected, ready=None):
                for t in range(NT):
                    if ready:
                        ready(t)
                    step_no_wait(nc.vector.bn_stats(stats[:, t, :], src[:, t, :]))
                dve.wait_ge(dve_step, n_step[0])
                m0, m1, c0, c1 = stats[:, :, 1], stats[:, :, 4], stats[:, :, 2], stats[:, :, 5]
                step(nc.vector.tensor_tensor(stat[:, 2, :], m0, m1, ALU.add))
                step(nc.vector.tensor_tensor(stat[:, 3, :], m0, m1, ALU.subtract))
                step(nc.vector.tensor_tensor(stat[:, 4, :], c0, c1, ALU.add))
                step(nc.vector.tensor_scalar(stat[:, 0, :], stat[:, 2, :], 0.5, None, ALU.mult))
                step(nc.vector.scalar_tensor_tensor(out=stat[:, 5, :], in0=stat[:, 3, :], scalar=0.25,
                                                    in1=stat[:, 3, :], op0=ALU.mult, op1=ALU.mult))
                step(nc.vector.scalar_tensor_tensor(out=stat[:, 2, :], in0=stat[:, 4, :], scalar=1.0 / D,
                                                    in1=stat[:, 5, :], op0=ALU.mult, op1=ALU.add))
                step(nc.vector.tensor_scalar(stat[:, 6, :], stat[:, 2, :], eps, None, ALU.add))
                assert n_step[0] == expected, (n_step[0], expected)

            def rstd(n):
                dve.wait_ge(a_rstd, n)
                step(nc.vector.reciprocal(stat[:, 1, :], stat[:, 7, :]))

            stats_a = take(NT * 6, numlo_at).rearrange("p (t k) -> p t k", k=6)
            variance(xn, stats_a, LN_EPS, A_VAR,
                     ready=lambda t: dve.wait_ge(in_x, 64) if t == 0 else None)
            rstd(1)
            for t in range(NT):
                step_no_wait(nc.vector.tensor_scalar(xn[:, t, :], xn[:, t, :], stat[:, 0, t:t + 1],
                                                     stat[:, 1, t:t + 1], ALU.subtract, ALU.mult))
            xn_ready = n_step[0]
            assert xn_ready == XN_READY, xn_ready
            dve.wait_ge(in_small, 8 * 16)
            step_no_wait(nc.vector.tensor_scalar(bq8, bq8, K ** -0.5, None, ALU.mult))
            dve.wait_ge(pool_const, 6)
            for n in range(HP):
                step_no_wait(nc.vector.tensor_scalar(bv_rows[:, n, :], ones[:, 0:P], bv_c[:, n:n + 1], None, ALU.mult))
            for r in range(4):
                for h in range(2):
                    step_no_wait(nc.vector.tensor_scalar(stack[K:K + 2, r, h, K2, :], ones[K:K + 2, 0:S],
                                                         ident[K:K + 2, K + h:K + h + 1], ROW_SCALE,
                                                         ALU.mult, ALU.mult))
            assert n_step[0] == SMALL_READY, n_step[0]
            dve.wait_ge(act_step, 4)
            for dst, hi_, raw, scale in ((wq_lo, wq_hi, raw_q, K ** -0.5), (wk_lo, wk_hi, raw_k, 1.0),
                                         (wv_lo, wv_hi, raw_v, 1.0), (wo_lo, wo_hi, raw_o, 1.0)):
                step_no_wait(nc.vector.scalar_tensor_tensor(
                    out=dst, in0=raw.rearrange("p (n c) -> p n c", n=HP), scalar=scale, in1=hi_,
                    op0=ALU.mult, op1=ALU.subtract))
            dve.wait_ge(act_step, 6)
            step_no_wait(nc.vector.tensor_tensor(router_lo, ps8[6][:, 0:E], router_hi, ALU.subtract))
            dve.wait_ge(bias_done, 1)
            step_no_wait(nc.vector.tensor_tensor(attn_bias, ps8[7][:, 0:D], bo_b, ALU.add))
            assert n_step[0] == A_DONE, n_step[0]

            def lo_block(n, ready, done):
                dve.wait_ge(ready, n + 1)
                nc.vector.tensor_tensor(xT_lo[:, n * S:(n + 1) * S], ps8[n % 4], xT_hi[:, n * S:(n + 1) * S],
                                        ALU.subtract).then_inc(done, 1)

            for n in range(B):
                lo_block(n, tr_a_hi, tr_a_lo)

            def run(p, u, batch):
                t = p + 3

                def row_max(s, h):
                    pair, q, up = p + 1 + (s + 2) // 4, (s + 2) % 4, u + 1 + (s + 2) // 4
                    if not valid(pair):
                        return
                    dve.wait_ge(max_scores, 8 * pair + 2 * q + h + 1)
                    if q == 0 and h == 0:
                        wait(dve, negmax_done, pair - 1)
                    nc.vector.tensor_reduce(rmax[:, up % 2, q, h:h + 1], ps_max, AX.X, ALU.max).then_inc(max_done, 1)
                    if q == 3 and h == 1:
                        dve.wait_ge(max_done, 8 * pair + 8)
                        wait(dve, maxrow_ps, pair - 1)
                        nc.vector.tensor_scalar(negmax[:, up % 2, :, :], rmax[:, up % 2, :, :], -1.0 / ROW_SCALE,
                                                EXP_SHIFT / ROW_SCALE, ALU.mult, ALU.add).then_inc(negmax_done, 1)

                for s in range(4):
                    if s == 0 and valid(p, -3):
                        _, b = batch_of(u, batch, -3)
                        dve.wait_ge(y_ps, p - 3 + 1)
                        wait(dve, y_added, p - 3)
                        dst = xn[:, bass.ds(b * QT, QT), :] if not isinstance(b, int) else xn[:, b * QT:b * QT + QT, :]
                        nc.vector.tensor_tensor(dst, ps_turn.rearrange("p (t d) -> p t d", t=QT), dst,
                                                ALU.add).then_inc(y_added, 1)
                    row_max(s, 0)
                    if valid(p, -1):
                        dve.wait_ge(ctx_ps, 4 * (p - 1) + s + 1)
                        wait(dve, ctx_done, 4 * (p - 1) + s - 1)
                        nc.vector.reciprocal(rden[:, s % 2, :], ps_ctx[:, K:K + P + 1:P]).then_inc(rden_done, 1)
                    if s == 3 and valid(p):
                        dve.wait_ge(exp_done, 4 * p + 2)
                        nc.vector.tensor_tensor(num_lo[:, u % 2, 1, :, :], num[:, u % 2, 1, :, :],
                                                num_hi[:, u % 2, 1, :, :, 1], ALU.subtract).then_inc(lo_dve, 1)
                    if s == 1 and valid(p, -2):
                        dve.wait_ge(ctx_hi, p - 2 + 1)
                        nc.vector.tensor_tensor(ctxT_lo[:, u % 2, :], ps_turn, ctxT_hi[:, u % 2, :],
                                                ALU.subtract).then_inc(ctx_lo, 1)
                    row_max(s, 1)
                    if s < 2 and valid(t):
                        n = batch_of(u, batch, 3)[0]
                        dve.wait_ge(qk_hi, 2 * t + s + 1)
                        nc.vector.scalar_tensor_tensor(out=flat[:, (u + 3) % 2, (ZQL, ZKL)[s], :], in0=ps_proj,
                                                       scalar=(bq8, bk_c)[s][:, n:n + 1],
                                                       in1=flat[:, (u + 3) % 2, (ZQH, ZKH)[s], :],
                                                       op0=ALU.add, op1=ALU.subtract).then_inc(qk_lo, 1)
                    if s == 2 and valid(p):
                        dve.wait_ge(v_hi_done, p + 1)
                        nc.vector.tensor_tensor(v_lo[:, u % 2, :, :, :],
                                                ps_proj.rearrange("p (t h c) -> p t h c", t=QT, h=2),
                                                v_hi[:, u % 2, :, :, 0:K], ALU.subtract).then_inc(v_lo_done, 1)

            steps(run, dve)

            def all_tiles(row):
                return row.unsqueeze(1).broadcast_to([P, NT, row.shape[1]])

            stats_c = take(NT * 6, wqkv_at).rearrange("p (t k) -> p t k", k=6)
            dve.wait_ge(y_added, PAIRS)
            step(nc.vector.tensor_tensor(xn, xn, all_tiles(attn_bias), ALU.add))
            variance(xn, stats_c, POST_EPS, C_VAR1)
            rstd(2)
            for t in range(NT):
                step_no_wait(nc.vector.tensor_scalar(xn[:, t, :], xn[:, t, :], stat[:, 0, t:t + 1],
                                                     stat[:, 1, t:t + 1], ALU.subtract, ALU.mult))
            dve.wait_ge(dve_step, n_step[0])
            step(nc.vector.tensor_tensor(xn, xn, all_tiles(gamma_b), ALU.mult))
            step(nc.vector.tensor_tensor(xn, xn, all_tiles(beta_b), ALU.add))
            dve.wait_ge(in_again, 16)
            step(nc.vector.tensor_tensor(xn, xn, x_again, ALU.add))
            variance(xn, stats_c, LN_EPS, C_VAR2)
            rstd(3)
            for t in range(NT):
                step_no_wait(nc.vector.tensor_scalar(xf[:, t, :], xn[:, t, :], stat[:, 0, t:t + 1],
                                                     stat[:, 1, t:t + 1], ALU.subtract, ALU.mult))
            assert n_step[0] == XF_READY, n_step[0]
            for n in range(B):
                lo_block(n, tr_c_hi, tr_c_lo)
            for n, (dst, raw, hi_) in enumerate(((gate_lo, raw_g, gate_hi), (up_lo, raw_u, up_hi), (down_lo, raw_d, down_hi))):
                dve.wait_ge(ffn_w_hi, n + 1)
                nc.vector.tensor_tensor(dst, raw, hi_, ALU.subtract).then_inc(ffn_w_lo, 2)

            dve.wait_ge(sigm, NT * E // 512)
            step(nc.vector.tensor_tensor(sfc, scores, all_tiles(ebias_b), ALU.add))
            g8 = sfc.rearrange("p t (g e) -> p (t g) e", g=G)
            n4, n2 = NT * G * 4, NT * G * 2
            hi4 = work1[:, 0:n4].rearrange("p (n e) -> p n e", e=4)
            lo4 = work1[:, n4:2 * n4].rearrange("p (n e) -> p n e", e=4)
            hi2, mid2, lo2, sec2 = (work2[:, i * n2:(i + 1) * n2].rearrange("p (n e) -> p n e", e=2) for i in range(4))
            step(nc.vector.tensor_tensor(hi4, g8[:, :, 0:4], g8[:, :, 4:8], ALU.max))
            step(nc.vector.tensor_tensor(lo4, g8[:, :, 0:4], g8[:, :, 4:8], ALU.min))
            step(nc.vector.tensor_tensor(hi2, hi4[:, :, 0:2], hi4[:, :, 2:4], ALU.max))
            step(nc.vector.tensor_tensor(mid2, hi4[:, :, 0:2], hi4[:, :, 2:4], ALU.min))
            step(nc.vector.tensor_tensor(lo2, lo4[:, :, 0:2], lo4[:, :, 2:4], ALU.max))
            step(nc.vector.tensor_tensor(sec2, mid2, lo2, ALU.max))
            n1 = NT * G
            hi1, mid1, lo1, sec1, gsum, rank = (work1[:, i * n1:(i + 1) * n1] for i in range(6))
            step(nc.vector.tensor_tensor(hi1, hi2[:, :, 0], hi2[:, :, 1], ALU.max))
            step(nc.vector.tensor_tensor(mid1, hi2[:, :, 0], hi2[:, :, 1], ALU.min))
            step(nc.vector.tensor_tensor(lo1, sec2[:, :, 0], sec2[:, :, 1], ALU.max))
            step(nc.vector.tensor_tensor(sec1, mid1, lo1, ALU.max))
            step(nc.vector.tensor_tensor(gsum, hi1, sec1, ALU.add))
            mine = gsum.rearrange("p (t g) -> p t g", t=NT).unsqueeze(3).broadcast_to([P, NT, G, G])
            other = gsum.rearrange("p (t g) -> p t g", t=NT).unsqueeze(2).broadcast_to([P, NT, G, G])
            w3 = work3.rearrange("p (t g h) -> p t g h", t=NT, g=G)
            w4 = work4.rearrange("p (t g h) -> p t g h", t=NT, g=G)
            dve.wait_ge(tr_c, B)
            step(nc.vector.tensor_tensor(w3, other, mine, ALU.is_ge))
            step(nc.vector.tensor_tensor(work3.rearrange("p (t n) -> p t n", t=NT), work3.rearrange("p (t n) -> p t n", t=NT),
                                         all_tiles(tri), ALU.mult))
            step(nc.vector.tensor_tensor(w4, other, mine, ALU.is_gt))
            step(nc.vector.tensor_tensor(work3, work3, work4, ALU.max))
            step(nc.vector.tensor_reduce(rank, work3.rearrange("p (n h) -> p n h", h=G), AX.X, ALU.add))
            step(nc.vector.tensor_scalar(rank, rank, float(TOPG) - 0.5, None, ALU.is_lt))
            masked = work4.rearrange("p (t e) -> p t e", t=NT)
            step(nc.vector.tensor_tensor(work4.rearrange("p (n e) -> p n e", e=EG), g8,
                                         rank.unsqueeze(2).broadcast_to([P, NT * G, EG]), ALU.mult))
            best = work2[:, 0:NT * TOPK].rearrange("p (t k) -> p t k", t=NT)
            for t in range(NT):
                step_no_wait(nc.vector.max(best[:, t, :], masked[:, t, :]))
            dve.wait_ge(dve_step, n_step[0])
            taken = work3.rearrange("p (t e) -> p t e", t=NT)
            for t in range(NT):
                step_no_wait(nc.vector.match_replace(taken[:, t, :], best[:, t, :], masked[:, t, :], -3.0e38))
            dve.wait_ge(dve_step, n_step[0])
            step(nc.vector.tensor_scalar(work3, work3, -2.0e38, None, ALU.is_lt))
            step(nc.vector.tensor_tensor(scores, scores, taken, ALU.mult))
            total, share = stat[:, 2, :], stat[:, 3, :]
            step(nc.vector.tensor_reduce(total, scores, AX.X, ALU.add))
            step(nc.vector.tensor_scalar(total, total, 1e-20, None, ALU.add))
            step(nc.vector.reciprocal(share, total))
            step(nc.vector.tensor_scalar(share, share, ROUTE_SCALE, None, ALU.mult))
            step(nc.vector.tensor_tensor(scores, scores, share.unsqueeze(2).broadcast_to([P, NT, E]), ALU.mult))
            both = f16(work1).rearrange("p (t k e) -> p t k e", t=NT, k=2)
            step(nc.vector.tensor_copy(both[:, :, 0, :], scores))
            step(nc.vector.tensor_tensor(both[:, :, 1, :], scores, both[:, :, 0, :], ALU.subtract))
            assert n_step[0] == COEF_READY, n_step[0]

            def tile(t, r, shared):
                dve.wait_ge(uc_ps, t + 1)
                dve.wait_ge(silu_done, t + 1)
                if not shared:
                    wait(dve, hid_done, t - 1)
                    nc.vector.tensor_tensor(prod[:, r % 2, :], silu_g[:, r % 2, :], ps8[2 + r % 2],
                                            ALU.mult).then_inc(prod_done, 1)
                    dve.wait_ge(prod_done, t + 1)
                wait(dve, hid_lo_done, t - 2)
                if shared:
                    nc.vector.tensor_tensor(hid[:, r % 3, :], silu_g[:, r % 2, :], ps8[2 + r % 2],
                                            ALU.mult).then_inc(hid_done, 1)
                    dve.wait_ge(hid_done, t + 1)
                    nc.vector.tensor_copy(prod[:, r % 2, 0:2], silu_g[:, r % 2, 0:2]).then_inc(prod_done, 1)
                else:
                    nc.vector.tensor_tensor(hid[:, r % 3, :], prod[:, r % 2, :], ps8[4 + r % 2],
                                            ALU.mult).then_inc(hid_done, 1)

            def finish(n):
                dve.wait_ge(down_done, TILES * (n + 1))
                nc.vector.tensor_copy(ysb, ps8[6]).then_inc(y_copied, 1)
                dve.wait_ge(y_back, n + 1)
                x2 = xn[:, bass.ds(n * QT, QT), :] if not isinstance(n, int) else xn[:, n * QT:(n + 1) * QT, :]
                nc.vector.tensor_tensor(x2, ps8[7].rearrange("p (t d) -> p t d", t=QT), x2,
                                        ALU.add).then_inc(out_ready, 1)

            def blocks(n, r):
                t0 = n * TILES
                with dve.Fori(0, 5) as k:
                    for i in range(6):
                        tile(k * 6 + (t0 + 3 + i), (TILES * r + 3 + i) % 6, False)
                if not (isinstance(n, int) and n == B - 1):
                    for i in range(3):
                        tile(t0 + TILES + i, (TILES * (r + 1) + i) % 6, i == 0)
                finish(n)

            for i in range(3):
                tile(i, i, i == 0)
            with dve.Fori(0, B // 2 - 1) as n2:
                for r in range(2):
                    blocks(n2 * 2 + r, r)
            for r in range(2):
                blocks(B - 2 + r, r)

        @block.tensor
        def _(pe):
            def mm(out_, lhsT, rhs, start, stop):
                return nc.tensor.matmul(out_, lhsT, rhs, start=start, stop=stop, skip_group_check=True)

            def product(out_, a_hi, a_lo, b_hi, b_lo, start=True, stop=True):
                mm(out_, a_hi, b_hi, start, False)
                mm(out_, a_hi, b_lo, False, False)
                return mm(out_, a_lo, b_hi, False, stop)

            pe.wait_ge(pool_const, 2)
            pe.wait_ge(in_small, 8 * 16)
            nc.tensor.transpose(ps8[6][:, 0:E], router_raw[0:E, :], ident[0:E, 0:E]).then_inc(router_t, 1)
            pe.wait_ge(in_w, 64)
            pe.wait_ge(dve_step, SMALL_READY)
            for n in range(HP):
                last = mm(ps8[7][:, 0:D], bv_rows[:, n, :], raw_o[:, n * D:(n + 1) * D], n == 0, n == HP - 1)
            last.then_inc(bias_done, 1)

            def transposes(src, done, lo_done):
                for n in range(B):
                    if n >= 4:
                        pe.wait_ge(lo_done, n - 3)
                    for t in range(QT):
                        last = nc.tensor.transpose(ps8[n % 4][:, t * P:(t + 1) * P], src[:, n * QT + t, :], ident)
                    last.then_inc(done, 1)

            pe.wait_ge(dve_step, XN_READY)
            transposes(xn, tr_a, tr_a_lo)
            pe.wait_ge(dve_step, A_DONE)
            pe.wait_ge(tr_a_lo, B)
            pe.wait_ge(act_step, 6)

            def tokens(xT, b, off=0, n=S):
                return xT[:, bass.ds(b * S + off, n)] if not isinstance(b, int) else xT[:, b * S + off:b * S + off + n]

            def run(p, u, batch):
                t = p + 3

                def query_tile(s, h):
                    pair, q, up = p + 1 + (s + 2) // 4, (s + 2) % 4, u + 1 + (s + 2) // 4
                    if not valid(pair):
                        return
                    if q == 0 and h == 0:
                        half = (p + 2) // 2 if isinstance(p, int) else batch * (HP // 2) + (u + 2) // 2
                        pe.wait_ge(stacked[up % 2], 96 * (half + 1))
                    wait(pe, max_done, 8 * pair + 2 * q + h)
                    st = stack[:, up % 4, h, :, :]
                    mm(ps_max, st[:, Q1, q * P:(q + 1) * P], st[:, K1, :], True, True).then_inc(max_scores, 1)

                for s in range(4):
                    if valid(p):
                        if s == 0:
                            pe.wait_ge(maxrow, p + 1)
                        wait(pe, exp_done, 4 * p + s - 1)
                        ks = slice(s * P, (s + 1) * P)
                        for h in range(2):
                            o = ps_st[s % 2][:, h * S:(h + 1) * S]
                            st = stack[:, u % 4, h, :, :]
                            mm(o, st[:, K1, ks], st[:, Q1, :], True, False)
                            last = mm(o, st[0:K + 2, K2, ks], st[0:K + 2, Q2, :], False, True)
                        last.then_inc(scores_t, 1)
                    query_tile(s, 0)
                    if s == 2 and valid(p, 1):
                        wait(pe, ctx_lo, p - 2 + 1)
                        if isinstance(p, int):
                            wait(pe, maxrow, p + 1)
                        pe.wait_ge(negmax_done, p + 1 + 1)
                        for k in range(QT):
                            last = mm(ps_turn[K:K + 2, k * P:(k + 1) * P], negmax[:, (u + 1) % 2, k, :], ident16, True, True)
                        last.then_inc(maxrow_ps, 1)
                    if valid(p, -1):
                        h, q0, o = s // 2, 2 * (s % 2), (u + 1) % 2
                        wait(pe, ctx_done, 4 * (p - 1) + s)
                        if s == 0:
                            pe.wait_ge(v_lo_done, p)
                            pe.wait_ge(lo_dve, p)
                            pe.wait_ge(lo_pool, 3 * (p - 1) + 2)
                        for k in range(QT):
                            if s == 0 and k == QT - 1:
                                pe.wait_ge(lo_pool, 3 * (p - 1) + 3)
                            for q in range(2):
                                qs = slice((q0 + q) * P, (q0 + q + 1) * P)
                                c = ps_ctx[:, q * P:q * P + K + 1]
                                mm(c, num_hi[:, o, k, h, qs, 1], v_hi[:, o, k, h, :], k == 0 and q == 0, False)
                                mm(c[:, 0:K], num_hi[:, o, k, h, qs, 1], v_lo[:, o, k, h, :], False, False)
                                last = mm(c, num_lo[:, o, k, h, qs], v_hi[:, o, k, h, :], False, k == QT - 1)
                        last.then_inc(ctx_ps, 1)
                    if s < 2 and valid(t):
                        n, b = batch_of(u, batch, 3)
                        w_hi, w_lo = ((wq_hi, wq_lo), (wk_hi, wk_lo))[s]
                        if s == 0:
                            wait(pe, v_lo_done, p)
                            if isinstance(t, int):
                                wait(pe, qk_lo, 2 * t)
                        else:
                            pe.wait_ge(qk_lo, 2 * t + 1)
                        product(ps_proj, w_hi[:, n, :], w_lo[:, n, :], tokens(xT_hi, b), tokens(xT_lo, b)).then_inc(qk_proj, 1)
                    if s == 2 and valid(p):
                        n, b = batch_of(u, batch, 0)
                        pe.wait_ge(qk_lo, upto(2 * t + 2, 2 * PAIRS))
                        for k in range(QT):
                            last = product(ps_proj[:, k * P:(k + 1) * P], tokens(xT_hi, b, k * P, P), tokens(xT_lo, b, k * P, P),
                                           wv_hi[:, n, :], wv_lo[:, n, :])
                        last.then_inc(v_proj, 1)
                    if s == 3 and valid(p, -2):
                        n, _ = batch_of(u, batch, -2)
                        pe.wait_ge(ctx_lo, p - 2 + 1)
                        pe.wait_ge(maxrow, upto(p + 1 + 1, PAIRS))
                        for k in range(QT):
                            ks = slice(k * P, (k + 1) * P)
                            last = product(ps_turn[:, ks], ctxT_hi[:, u % 2, ks], ctxT_lo[:, u % 2, ks],
                                           wo_hi[:, n, :], wo_lo[:, n, :])
                        last.then_inc(y_ps, 1)
                    query_tile(s, 1)
                    if s == 0 and valid(p, -2):
                        wait(pe, y_added, p - 2)
                        if isinstance(p, int):
                            wait(pe, maxrow, upto(p + 1, PAIRS))
                        pe.wait_ge(ctx_done, 4 * (p - 2) + 4)
                        for k in range(QT):
                            last = nc.tensor.transpose(ps_turn[:, k * P:(k + 1) * P], ctxn[:, u % 2, k, :], ident)
                        last.then_inc(ctx_t, 1)

            steps(run, pe)

            pe.wait_ge(dve_step, XF_READY)
            transposes(xf, tr_c, tr_c_lo)
            for t in range(NT):
                if t % 4 == 0:
                    pe.wait_ge(tr_c_lo, t // 4 + 1)
                ts_ = slice(t * P, (t + 1) * P)
                last = product(ps8[4 + t // 8][:, (t % 8) * E:(t % 8 + 1) * E], xT_hi[:, ts_], xT_lo[:, ts_], router_hi, router_lo)
                if t % 8 == 7:
                    last.then_inc(logits, 1)
            pe.wait_ge(dve_step, COEF_READY)
            both = f16(work1).rearrange("p (t n) -> p t n", t=NT)
            for n in range(NT // 4):
                if n >= 4:
                    pe.wait_ge(coef_sb, n - 3)
                for k in range(4):
                    last = nc.tensor.transpose(ps8[n % 4].bitcast(F16)[:, k * P:(k + 1) * P], both[:, 4 * n + k, :], ident16)
                last.then_inc(coef_t, 1)
            pe.wait_ge(coef_sb, NT // 4)
            pe.wait_ge(ffn_w_lo, 6)
            pe.wait_ge(sel_done, 3)
            pe.wait_ge(sigm, NT * E // 512)

            def weights(w, k):
                return w[:, k, :] if isinstance(k, int) else w[:, bass.ds(k, 1), :].rearrange("p o n -> p (o n)")

            def gate_up(t, r, k, b):
                wait(pe, silu_done, t - 1)
                product(ps8[r % 2], weights(gate_hi, k), weights(gate_lo, k), tokens(xT_hi, b), tokens(xT_lo, b)).then_inc(g_ps, 1)
                wait(pe, hid_done, t - 1)
                last = product(ps8[2 + r % 2], weights(up_hi, k), weights(up_lo, k), tokens(xT_hi, b), tokens(xT_lo, b))
                if not (isinstance(k, int) and k == 0):
                    s = (sel[:, k - 1, :, :] if isinstance(k, int) else sel[:, bass.ds(k - 1, 1), :, :].rearrange("p o h m -> p (o h m)"))
                    if isinstance(k, int):
                        s = s.rearrange("p h m -> p (h m)")
                    last = mm(ps8[4 + r % 2], s, tokens(coefT, b), True, True)
                last.then_inc(uc_ps, 1)

            def down(t, r, k):
                pe.wait_ge(hid_lo_done, t + 1)
                first = isinstance(k, int) and k == 0
                product(ps8[6], weights(down_hi, k), weights(down_lo, k), hid_hi[:, r % 3, :], hid_lo[:, r % 3, :],
                        start=first, stop=isinstance(k, int) and k == TILES - 1).then_inc(down_done, 1)

            def block_of(n, r):
                t0 = n * TILES
                gate_up(t0 + 3, (TILES * r + 3) % 6, 3, n)
                down(t0, (TILES * r) % 6, 0)
                for i in range(1, 6):
                    gate_up(t0 + 3 + i, (TILES * r + 3 + i) % 6, 3 + i, n)
                    down(t0 + i, (TILES * r + i) % 6, i)
                with pe.Fori(1, 5) as k:
                    for i in range(6):
                        gate_up(k * 6 + (t0 + 3 + i), (TILES * r + 3 + i) % 6, k * 6 + (3 + i), n)
                        down(k * 6 + (t0 + i), (TILES * r + i) % 6, k * 6 + i)
                for i in range(3):
                    if not (isinstance(n, int) and n == B - 1):
                        gate_up(t0 + TILES + i, (TILES * (r + 1) + i) % 6, i, n + 1)
                    down(t0 + 30 + i, (TILES * r + 30 + i) % 6, 30 + i)
                pe.wait_ge(y_copied, n + 1)
                for k in range(QT):
                    last = nc.tensor.transpose(ps8[7][:, k * P:(k + 1) * P], ysb[:, k * P:(k + 1) * P], ident)
                last.then_inc(y_back, 1)

            for i in range(3):
                gate_up(i, i, i, 0)
            with pe.Fori(0, B // 2 - 1) as n2:
                for r in range(2):
                    block_of(n2 * 2 + r, r)
            for r in range(2):
                block_of(B - 2 + r, r)


_VAR = NT + 7
A_VAR = _VAR
XN_READY = A_VAR + 1 + NT
SMALL_READY = XN_READY + 1 + HP + 8
A_DONE = SMALL_READY + 6
C_VAR1 = A_DONE + 1 + _VAR
C_VAR2 = C_VAR1 + 1 + NT + 3 + _VAR
XF_READY = C_VAR2 + 1 + NT
COEF_READY = XF_READY + 12 + 7 + 2 * NT + 9

_INS = ["x", "Wq", "bq", "Wk", "bk", "Wv", "bv", "Wo", "bo", "gamma", "beta"]
_FFN = ["router_w", "e_bias", "Wg", "Wu", "Wd", "SWg", "SWu", "SWd"]


def kernel(**inputs):
    import numpy as np
    import concourse.bacc as bacc
    from concourse.bass_utils import run_bass_kernel_spmd

    nc = bacc.Bacc("TRN2", target_bir_lowering=False, num_devices=1)
    arrays, args = {}, []
    for name in ["L0_attn_" + n for n in _INS] + ["L0_ffn_" + n for n in _FFN]:
        a = np.ascontiguousarray(inputs[name])
        arrays[f"in_{name}"] = a
        args.append(nc.dram_tensor(f"in_{name}", a.shape, mybir.dt.from_np(a.dtype), kind="ExternalInput").ap())
    out = nc.dram_tensor("out_0", (B, S, D), F32, kind="ExternalOutput").ap()
    layer(nc, *args, out)
    result = run_bass_kernel_spmd(nc, [arrays], core_ids=[0])
    return result.results[0]["out_0"]
```

```python
from contextlib import ExitStack

import concourse.bass as bass
from concourse import mybir

P = 128
F32 = mybir.dt.float32
F16 = mybir.dt.float16
BF16 = mybir.dt.bfloat16
ALU = mybir.AluOpType
ACT = mybir.ActivationFunctionType
AX = mybir.AxisListType

B, S, D = 8, 512, 128
H, K = 16, 64
HP = H // 2
PAIRS = B * HP
QT = S // P
TOK = B * S
NT = TOK // P
E, G, TOPG, TOPK = 64, 8, 4, 8
EG = E // G
EP = E // 2
TILES = EP + 1
ROUTE_SCALE = 2.5
LN_EPS, POST_EPS = 1e-5, 1e-3
ROW_SCALE = 1024.0
EXP_SHIFT = 5.0
Q1, Q2, K1, K2 = range(4)
ZQH, ZQL, ZKH, ZKL = range(4)
UNROLL = HP
FIRST, LAST = 4, 60


def layer(nc, x, Wq, bq, Wk, bk, Wv, bv, Wo, bo, gamma, beta, router_w, e_bias,
          Wg, Wu, Wd, SWg, SWu, SWd, out):
    with ExitStack() as ctx:
        def sem(name):
            return ctx.enter_context(nc.semaphore(name))

        ARENA = 53100
        arena = ctx.enter_context(nc.sbuf_tensor("arena", [P, ARENA], F32))
        top = [0]

        def take(words, at=None):
            if at is None:
                at = top[0]
                top[0] += words
                assert top[0] <= ARENA, top[0]
            return arena[:, at:at + words]

        def f16(ap):
            return ap.bitcast(F16)

        xn = take(NT * D).rearrange("p (t d) -> p t d", t=NT)
        xT_hi = f16(take(TOK // 2))
        xT_lo = f16(take(TOK // 2))
        ident = take(P)
        ident16 = f16(take(P // 2))
        gamma_b, beta_b, attn_bias = take(D), take(D), take(D)
        ebias_b = take(E)
        router_hi, router_lo = f16(take(E // 2)), f16(take(E // 2))
        bq8, bk_c, bv_c = take(HP), take(HP), take(HP)
        stat = take(8 * NT).rearrange("p (k t) -> p k t", k=8)
        half_pow = take(NT)
        tri = take(G * G)
        w_hi, w_lo = (f16(take(TILES * 3 * P // 2)).rearrange("p (t k n) -> p t k n", t=TILES, k=3) for _ in range(2))
        wqkv_at = top[0]
        wq_hi, wq_lo, wk_hi, wk_lo, wv_hi, wv_lo = (
            f16(take(H * K // 2)).rearrange("p (n c) -> p n c", n=HP) for _ in range(6))
        wo_hi, wo_lo = (f16(take(HP * D // 2)).rearrange("p (n c) -> p n c", n=HP) for _ in range(2))
        stack_at = top[0]
        stack = f16(take(4 * 2 * 4 * S // 2)).rearrange("p (r h k q) -> p r h k q", r=4, h=2, k=4)
        flat = f16(take(2 * 4 * S // 2)).rearrange("p (r k q) -> p r k q", r=2, k=4)
        v_hi = f16(take(2 * QT * 2 * (K + 1) // 2)).rearrange("p (r t h c) -> p r t h c", r=2, t=QT, h=2)
        v_lo = f16(take(2 * QT * 2 * K // 2)).rearrange("p (r t h c) -> p r t h c", r=2, t=QT, h=2)
        num_at = top[0]
        num_flat = take(2 * QT * 2 * S)
        num = num_flat.rearrange("p (r t h q) -> p r t h q", r=2, t=QT, h=2)
        num_hi = num_flat.bitcast(BF16).rearrange("p (r t h q w) -> p r t h q w", r=2, t=QT, h=2, w=2)
        numlo_at = top[0]
        num_lo = f16(take(2 * QT * 2 * S // 2)).rearrange("p (r t h q) -> p r t h q", r=2, t=QT, h=2)
        ctxn = take(2 * QT * P).rearrange("p (r t c) -> p r t c", r=2, t=QT)
        ctxT_hi = f16(take(2 * S // 2)).rearrange("p (r q) -> p r q", r=2)
        ctxT_lo = f16(take(2 * S // 2)).rearrange("p (r q) -> p r q", r=2)
        rmax = take(2 * QT * 2).rearrange("p (r t h) -> p r t h", r=2, t=QT)
        negmax = f16(take(2 * QT)).rearrange("p (r t h) -> p r t h", r=2, t=QT)
        rden = take(2 * 2).rearrange("p (r t) -> p r t", r=2)
        w_raw = take(2 * 3 * P).rearrange("p (r k n) -> p r k n", r=2, k=3)
        raw_q, raw_k, raw_v, raw_o = (take(H * K, num_at + i * H * K) for i in range(4))
        bv_rows = take(HP * P, num_at + 4 * H * K).rearrange("p (n c) -> p n c", n=HP)
        router_raw = take(D, num_at + 5 * H * K)
        bo_b = take(D, num_at + 5 * H * K + D)
        ones = take(S, num_at + 5 * H * K + 2 * D)
        top[0] = stack_at
        sel = f16(take(EP * P // 2)).rearrange("p (j h m) -> p j h m", j=EP, h=2)
        xin = take(2 * S).rearrange("p (r t d) -> p r t d", r=2, t=QT)
        x2 = take(2 * S).rearrange("p (r t d) -> p r t d", r=2, t=QT)
        ya = take(S).rearrange("p (t d) -> p t d", t=QT)
        xf = take(S).rearrange("p (t d) -> p t d", t=QT)
        fT_hi, fT_lo, coefT = (f16(take(2 * S // 2)).rearrange("p (r q) -> p r q", r=2) for _ in range(3))
        bn = take(QT * 6).rearrange("p (t k) -> p t k", t=QT)
        mean_var = take(QT * 2).rearrange("p (t k) -> p t k", t=QT)
        veps, rstd = take(QT), take(QT)
        scores, sfc = (take(QT * E).rearrange("p (t e) -> p t e", t=QT) for _ in range(2))
        work1, work2, work3, work4 = (take(QT * E) for _ in range(4))
        both = f16(take(QT * E)).rearrange("p (t k e) -> p t k e", t=QT, k=2)
        total, share = take(QT), take(QT)
        silu_g = take(2 * S).rearrange("p (r q) -> p r q", r=2)
        prod = take(2 * S).rearrange("p (r q) -> p r q", r=2)
        hid = take(3 * S).rearrange("p (r q) -> p r q", r=3)
        hid_hi, hid_lo = (f16(take(3 * S // 2)).rearrange("p (r q) -> p r q", r=3) for _ in range(2))
        ysb = take(S)

        bank = [ctx.enter_context(nc.psum_tensor(f"bank{i}", [P, 1024], F32)) for i in range(4)]
        ps_st = [bank[0], bank[1]]
        ps8 = [bank[i // 2][:, (i % 2) * 512:(i % 2) * 512 + 512] for i in range(8)]
        ps_max = ps8[4]
        ps_ctx = ps8[5]
        ps_proj = ps8[6]
        ps_turn = ps8[7]

        in_x = sem("in_x")
        in_w = sem("in_w")
        in_small = sem("in_small")
        w_in = [sem("w_in0"), sem("w_in1")]
        w_hi_done = sem("w_hi_done")
        w_split = sem("w_split")
        dve_step = sem("dve_step")
        act_step = sem("act_step")
        pool_const = sem("pool_const")
        tr_a = sem("tr_a")
        tr_a_hi = sem("tr_a_hi")
        tr_a_lo = sem("tr_a_lo")
        bias_done = sem("bias_done")
        router_t = sem("router_t")
        a_rstd = sem("a_rstd")
        qk_proj = sem("qk_proj")
        qk_hi = sem("qk_hi")
        qk_lo = sem("qk_lo")
        v_proj = sem("v_proj")
        v_hi_done = sem("v_hi_done")
        v_lo_done = sem("v_lo_done")
        stacked = [sem("stacked0"), sem("stacked1")]
        max_scores = sem("max_scores")
        max_done = sem("max_done")
        negmax_done = sem("negmax_done")
        maxrow_ps = sem("maxrow_ps")
        maxrow = sem("maxrow")
        scores_t = sem("scores_t")
        exp_done = sem("exp_done")
        lo_pool = sem("lo_pool")
        ctx_ps = sem("ctx_ps")
        rden_done = sem("rden_done")
        ctx_done = sem("ctx_done")
        ctx_t = sem("ctx_t")
        ctx_hi = sem("ctx_hi")
        ctx_lo = sem("ctx_lo")
        y_ps = sem("y_ps")
        y_added = sem("y_added")
        x_in = [sem("x_in0"), sem("x_in1")]
        xbeta = sem("xbeta")
        rstd_done = sem("rstd_done")
        c_var = sem("c_var")
        xf_done = sem("xf_done")
        tr_c = sem("tr_c")
        tr_c_hi = sem("tr_c_hi")
        tr_c_lo = sem("tr_c_lo")
        logits = sem("logits")
        sigm = sem("sigm")
        coef = sem("coef")
        sfc_done = sem("sfc_done")
        coef_t = sem("coef_t")
        coef_sb = sem("coef_sb")
        route_step = sem("route_step")
        sel_done = sem("sel_done")
        g_ps = sem("g_ps")
        uc_ps = sem("uc_ps")
        silu_done = sem("silu_done")
        prod_done = sem("prod_done")
        hid_done = sem("hid_done")
        hid_hi_done = sem("hid_hi_done")
        hid_lo_done = sem("hid_lo_done")
        down_done = sem("down_done")
        y_copied = sem("y_copied")
        y_back = sem("y_back")
        out_ready = sem("out_ready")
        out_sent = sem("out_sent")

        def wait(eng, s, value):
            if isinstance(value, int) and value <= 0:
                return
            eng.wait_ge(s, value)

        def upto(value, most):
            return min(value, most) if isinstance(value, int) else value

        def valid(pair, off=0):
            return not isinstance(pair, int) or 0 <= pair + off < PAIRS

        def steps(run, eng):
            for p in range(-3, FIRST):
                run(p, p % UNROLL, p // HP)
            with eng.Fori(0, (LAST - FIRST) // UNROLL) as i:
                for u in range(UNROLL):
                    run(i * UNROLL + (FIRST + u), (FIRST + u) % UNROLL, i + (FIRST + u) // HP)
            for p in range(LAST, PAIRS + 3):
                run(p, p % UNROLL, p // HP)

        def batch_of(u, batch, off):
            return (u + off) % HP, batch + (u + off) // HP

        def blocks(eng, run):
            with eng.Fori(0, B // 2 - 1) as i:
                for r in range(2):
                    run(i * 2 + r, r, False)
            for r in range(2):
                run(B - 2 + r, r, r == 1)

        block = ctx.enter_context(nc.Block())

        @block.sync
        def _(sp):
            xv = x.rearrange("b (t p) d -> p (b t) d", p=P)
            for c in range(4):
                n = NT // 4
                sp.dma_start(xn[:, c * n:(c + 1) * n, :], xv[:, c * n:(c + 1) * n, :]).then_inc(in_x, 16)
            sp.dma_start(raw_q, Wq.rearrange("d h k -> d (h k)")).then_inc(in_w, 16)
            sp.dma_start(raw_k, Wk.rearrange("d h k -> d (h k)")).then_inc(in_w, 16)
            sp.dma_start(raw_v, Wv.rearrange("d h k -> d (h k)")).then_inc(in_w, 16)
            sp.dma_start(raw_o.rearrange("p (n c) -> p n c", n=HP),
                         Wo.rearrange("h k d -> (h k) d").rearrange("(n p) d -> p n d", p=P)).then_inc(in_w, 16)
            with nc.allow_non_contiguous_dma(reason="small vectors"):
                for dst, src in ((bq8, bq), (bk_c, bk), (bv_c, bv)):
                    sp.dma_start(dst, src.rearrange("h k -> (h k)").rearrange("(n p) -> p n", p=P)).then_inc(in_small, 16)
                for dst, src in ((gamma_b, gamma), (beta_b, beta), (bo_b, bo), (ebias_b, e_bias)):
                    sp.dma_start(dst, src.partition_broadcast(P)).then_inc(in_small, 16)
            sp.dma_start(router_raw[0:E, :], router_w).then_inc(in_small, 16)

            for n, src in enumerate((SWg, SWu, SWd)):
                sp.dma_start(w_raw[:, 0, n, :], src).then_inc(w_in[0], 16)

            def run(p, u, batch):
                t = p + 3
                if valid(t):
                    wait(sp, scores_t, 4 * p)
                    r, z, odd = (u + 3) % 4, (u + 3) % 2, (u + 3) % 2
                    sp.wait_ge(qk_lo, 2 * t + 2)
                    for h in range(2):
                        a = flat[h * K:(h + 1) * K, z, :, :]
                        high, low = stack[0:K, r, h, :, :], stack[K:P, r, h, :, :]
                        sp.dma_start(high[:, Q1:Q2 + 1, :], a[:, ZQH:ZQH + 1, :].broadcast_to([K, 2, S])).then_inc(stacked[odd], 16)
                        sp.dma_start(high[:, K1:K2 + 1, :], a[:, ZKH:ZKL + 1, :]).then_inc(stacked[odd], 16)
                        sp.dma_start(low[:, Q1:K1 + 1:2, :], a[:, ZQL:ZKH + 1, :]).then_inc(stacked[odd], 16)

                w = p + 2
                if u % 2 == 0 and (not isinstance(w, int) or 0 <= w < PAIRS):
                    v, vb = batch_of(u, batch, 2)
                    tile, r = vb * (HP // 2) + v // 2 + 1, (v // 2 + 1) % 2
                    wait(sp, w_split, tile - 1)
                    j = tile - 1
                    e2 = slice(2 * j, 2 * j + 2) if isinstance(j, int) else bass.ds(j * 2, 2)
                    for n, src in enumerate((Wg, Wu)):
                        sp.dma_start(w_raw[:, r, n, :].rearrange("p (e i) -> p e i", e=2),
                                     src[e2].rearrange("e h i -> h e i")).then_inc(w_in[r], 16)
                    sp.dma_start(w_raw[:, r, 2, :], Wd[e2].rearrange("e i h -> (e i) h")).then_inc(w_in[r], 16)

            steps(run, sp)

            xv = x.rearrange("b (t p) d -> b p t d", p=P)
            ov = out.rearrange("b (t p) d -> b p t d", p=P)
            sp.wait_ge(scores_t, 4 * PAIRS)
            for m in range(B + 2):
                if m >= 2:
                    sp.wait_ge(out_ready, m - 1)
                    sp.dma_start(ov[m - 2], x2[:, m % 2, :, :]).then_inc(out_sent, 16)
                    sp.wait_ge(out_sent, 16 * (m - 1))
                if m < B:
                    sp.dma_start(xin[:, m % 2, :, :], xv[m]).then_inc(x_in[m % 2], 16)

        @block.gpsimd
        def _(pool):
            pool.memset(ident, 0.0).then_inc(pool_const, 1)
            pool.wait_ge(pool_const, 1)
            pool.affine_select(out=ident, in_=ident, compare_op=ALU.not_equal, fill=1.0, base=0,
                               pattern=[[-1, P]], channel_multiplier=1).then_inc(pool_const, 1)
            pool.memset(tri, 1.0).then_inc(pool_const, 1)
            pool.wait_ge(pool_const, 3)
            pool.affine_select(out=tri.rearrange("p (g h) -> p g h", g=G), in_=tri.rearrange("p (g h) -> p g h", g=G),
                               compare_op=ALU.is_gt, fill=0.0, base=0, pattern=[[1, G], [-1, G]],
                               channel_multiplier=0).then_inc(pool_const, 1)
            pool.memset(ones, 1.0).then_inc(pool_const, 1)
            pool.memset(v_hi[:, :, :, :, K:K + 1], 1.0).then_inc(pool_const, 1)
            pool.memset(half_pow, -0.5).then_inc(pool_const, 1)
            pool.wait_ge(pool_const, 7)
            pool.wait_ge(dve_step, A_VAR)
            pool.tensor_tensor(stat[:, 1, :], stat[:, 6, :], half_pow, ALU.pow).then_inc(a_rstd, 1)

            def run(p, u, batch):
                def lo(s):
                    pool.wait_ge(exp_done, 4 * p + s + 1)
                    if s == 0:
                        wait(pool, ctx_ps, 4 * (p - 2) + 4)
                    pool.tensor_tensor(num_lo[:, u % 2, s, :, :], num[:, u % 2, s, :, :],
                                       num_hi[:, u % 2, s, :, :, 1], ALU.subtract).then_inc(lo_pool, 1)

                if valid(p):
                    for s in range(4):
                        lo(s)

            steps(run, pool)

            pool.wait_ge(scores_t, 4 * PAIRS)
            pool.memset(sel, 0.0).then_inc(sel_done, 1)
            pool.wait_ge(sel_done, 1)
            for n, off in enumerate((0, E)):
                pool.affine_select(out=sel, in_=sel, compare_op=ALU.not_equal, fill=1.0, base=-off,
                                   pattern=[[-2, EP], [-1, 2], [0, E]], channel_multiplier=1).then_inc(sel_done, 1)
                pool.wait_ge(sel_done, 2 + n)

            def route(m, r, k):
                if k in (6, 11):
                    pool.wait_ge(c_var, m * 2 + (1 if k == 6 else 2))
                    pool.tensor_tensor(rstd, veps, half_pow[:, 0:QT], ALU.pow).then_inc(rstd_done, 1)
                if k == 19:
                    pool.wait_ge(sigm, m + 1)
                    pool.tensor_tensor(sfc, scores, ebias_b.unsqueeze(1).broadcast_to([P, QT, E]),
                                       ALU.add).then_inc(sfc_done, 1)
                if k == 7:
                    count = m // 2 + 1 if isinstance(m, int) else block_i[0] + (1 if r else 2)
                    pool.wait_ge(x_in[r], count * 16)
                    pool.tensor_tensor(xin[:, r, :, :], xin[:, r, :, :],
                                       beta_b.unsqueeze(1).broadcast_to([P, QT, D]), ALU.add).then_inc(xbeta, 1)

            def tile(t, r):
                pool.wait_ge(hid_hi_done, t + 1)
                wait(pool, down_done, t - 2)
                pool.tensor_tensor(hid_lo[:, r % 3, :], hid[:, r % 3, :], hid_hi[:, r % 3, :],
                                   ALU.subtract).then_inc(hid_lo_done, 1)

            block_i = [None]

            def run_block(n, r, last):
                for k in range(4, TILES if last else TILES + 4):
                    tile(n * TILES + k, (r * TILES + k) % 6)
                    if not last:
                        route(n + 1, 1 - r, k)

            for k in range(TILES + 4):
                route(0, 0, k)
            for t in range(4):
                tile(t, t)
            with pool.Fori(0, B // 2 - 1) as i:
                block_i[0] = i
                for r in range(2):
                    run_block(i * 2 + r, r, False)
            for r in range(2):
                run_block(B - 2 + r, r, r == 1)

        @block.scalar
        def _(act):
            n_act = [0]

            def step(ins):
                ins.then_inc(act_step, 1)
                n_act[0] += 1

            act.wait_ge(in_w, 64)
            act.wait_ge(in_small, 8 * 16)
            step(nc.scalar.activation(wq_hi, raw_q.rearrange("p (n c) -> p n c", n=HP), ACT.Copy, scale=K ** -0.5))
            step(nc.scalar.activation(wk_hi, raw_k.rearrange("p (n c) -> p n c", n=HP), ACT.Copy))
            step(nc.scalar.activation(wv_hi, raw_v.rearrange("p (n c) -> p n c", n=HP), ACT.Copy))
            step(nc.scalar.activation(wo_hi, raw_o.rearrange("p (n c) -> p n c", n=HP), ACT.Copy))
            act.wait_ge(pool_const, 2)
            step(nc.scalar.activation(ident16, ident, ACT.Copy))
            act.wait_ge(router_t, 1)
            step(nc.scalar.activation(router_hi, ps8[6][:, 0:E], ACT.Copy))

            def hi_block(n, ready, done):
                act.wait_ge(ready, n + 1)
                nc.scalar.activation(xT_hi[:, n * S:(n + 1) * S], ps8[n % 4], ACT.Copy).then_inc(done, 1)

            for n in range(B):
                hi_block(n, tr_a, tr_a_hi)

            def run(p, u, batch):
                t = p + 3

                def hi(which, n):
                    act.wait_ge(qk_proj, 2 * t + which + 1)
                    if which == 0 and (not isinstance(t, int) or t >= 2):
                        act.wait_ge(max_scores, 8 * (t - 2) + 1)
                    bias = (bq8, bk_c)[which]
                    nc.scalar.activation(flat[:, (u + 3) % 2, (ZQH, ZKH)[which], :], ps_proj, ACT.Identity,
                                         bias=bias[:, n:n + 1]).then_inc(qk_hi, 1)

                for s in range(4):
                    if valid(p):
                        act.wait_ge(scores_t, 4 * p + s + 1)
                        if s == 0:
                            wait(act, ctx_ps, 4 * (p - 2) + 4)
                        nc.scalar.activation(num[:, u % 2, s, :, :],
                                             ps_st[s % 2][:, :].rearrange("p (h q) -> p h q", h=2),
                                             ACT.Exp).then_inc(exp_done, 1)
                    if s == 2 and valid(p, 1):
                        act.wait_ge(maxrow_ps, p + 1 + 1)
                        nc.scalar.activation(stack[K:K + 2, (u + 1) % 4, :, Q2, :],
                                             ps_turn[K:K + 2, :].unsqueeze(1).broadcast_to([2, 2, S]),
                                             ACT.Copy).then_inc(maxrow, 1)
                    if valid(p, -1):
                        h, q0 = s // 2, 2 * (s % 2)
                        act.wait_ge(rden_done, 4 * (p - 1) + s + 1)
                        if s == 0:
                            wait(act, ctx_t, p - 3 + 1)
                        for q in range(2):
                            last = nc.scalar.activation(ctxn[:, (u + 1) % 2, q0 + q, h * K:(h + 1) * K],
                                                        ps_ctx[:, q * P:q * P + K], ACT.Copy,
                                                        scale=rden[:, s % 2, q:q + 1])
                        last.then_inc(ctx_done, 1)
                    if s == 0 and valid(t):
                        hi(0, batch_of(u, batch, 3)[0])
                    if s == 1 and valid(t):
                        hi(1, batch_of(u, batch, 3)[0])
                    if s == 2 and valid(p):
                        act.wait_ge(v_proj, p + 1)
                        wait(act, ctx_ps, 4 * (p - 2) + 4)
                        nc.scalar.activation(v_hi[:, u % 2, :, :, 0:K],
                                             ps_proj.rearrange("p (t h c) -> p t h c", t=QT, h=2),
                                             ACT.Copy).then_inc(v_hi_done, 1)
                    if s == 0 and valid(p, -2):
                        act.wait_ge(ctx_t, p - 2 + 1)
                        wait(act, y_ps, p - 4 + 1)
                        nc.scalar.activation(ctxT_hi[:, u % 2, :], ps_turn, ACT.Copy).then_inc(ctx_hi, 1)

            steps(run, act)

            def route(m, r, k):
                if k == 16:
                    act.wait_ge(tr_c, m + 1)
                    nc.scalar.activation(fT_hi[:, r, :], ps8[7], ACT.Copy).then_inc(tr_c_hi, 1)
                if k == 19:
                    act.wait_ge(logits, m + 1)
                    nc.scalar.activation(scores, ps8[7][:, 0:QT * E].rearrange("p (t e) -> p t e", t=QT), ACT.Sigmoid).then_inc(sigm, 1)
                if k == 32:
                    act.wait_ge(coef_t, m + 1)
                    nc.scalar.activation(coefT[:, r, :], ps8[7].bitcast(F16)[:, 0:S], ACT.Copy).then_inc(coef_sb, 1)

            def silu(t, r):
                act.wait_ge(g_ps, t + 1)
                wait(act, prod_done, t - 1)
                nc.scalar.activation(silu_g[:, r % 2, :], ps8[r % 2], ACT.Silu).then_inc(silu_done, 1)

            def hid_hi_tile(t, r):
                act.wait_ge(hid_done, t + 1)
                wait(act, down_done, t - 2)
                nc.scalar.activation(hid_hi[:, r % 3, :], hid[:, r % 3, :], ACT.Copy).then_inc(hid_hi_done, 1)

            def run_block(n, r, last):
                for k in range(4, TILES if last else TILES + 4):
                    silu(n * TILES + k, (r * TILES + k) % 6)
                    hid_hi_tile(n * TILES + (k - 1), (r * TILES + k - 1) % 6)
                    if not last:
                        route(n + 1, 1 - r, k)
                if last:
                    hid_hi_tile(n * TILES + (TILES - 1), (r * TILES + TILES - 1) % 6)

            for k in range(TILES + 4):
                route(0, 0, k)
            silu(0, 0)
            for t in range(1, 4):
                silu(t, t)
                hid_hi_tile(t - 1, t - 1)
            blocks(act, run_block)

        @block.vector
        def _(dve):
            n_step = [0]

            def step(ins):
                ins.then_inc(dve_step, 1)
                n_step[0] += 1
                dve.wait_ge(dve_step, n_step[0])

            def step_no_wait(ins):
                ins.then_inc(dve_step, 1)
                n_step[0] += 1

            def variance(src, stats, eps, expected, ready=None):
                for t in range(NT):
                    if ready:
                        ready(t)
                    step_no_wait(nc.vector.bn_stats(stats[:, t, :], src[:, t, :]))
                dve.wait_ge(dve_step, n_step[0])
                m0, m1, c0, c1 = stats[:, :, 1], stats[:, :, 4], stats[:, :, 2], stats[:, :, 5]
                step(nc.vector.tensor_tensor(stat[:, 2, :], m0, m1, ALU.add))
                step(nc.vector.tensor_tensor(stat[:, 3, :], m0, m1, ALU.subtract))
                step(nc.vector.tensor_tensor(stat[:, 4, :], c0, c1, ALU.add))
                step(nc.vector.tensor_scalar(stat[:, 0, :], stat[:, 2, :], 0.5, None, ALU.mult))
                step(nc.vector.scalar_tensor_tensor(out=stat[:, 5, :], in0=stat[:, 3, :], scalar=0.25,
                                                    in1=stat[:, 3, :], op0=ALU.mult, op1=ALU.mult))
                step(nc.vector.scalar_tensor_tensor(out=stat[:, 2, :], in0=stat[:, 4, :], scalar=1.0 / D,
                                                    in1=stat[:, 5, :], op0=ALU.mult, op1=ALU.add))
                step(nc.vector.tensor_scalar(stat[:, 6, :], stat[:, 2, :], eps, None, ALU.add))
                assert n_step[0] == expected, (n_step[0], expected)

            stats_a = take(NT * 6, numlo_at).rearrange("p (t k) -> p t k", k=6)
            variance(xn, stats_a, LN_EPS, A_VAR,
                     ready=lambda t: dve.wait_ge(in_x, 64) if t == 0 else None)
            dve.wait_ge(a_rstd, 1)
            for t in range(NT):
                step_no_wait(nc.vector.tensor_scalar(xn[:, t, :], xn[:, t, :], stat[:, 0, t:t + 1],
                                                     stat[:, 1, t:t + 1], ALU.subtract, ALU.mult))
            xn_ready = n_step[0]
            assert xn_ready == XN_READY, xn_ready
            dve.wait_ge(in_small, 8 * 16)
            step_no_wait(nc.vector.tensor_scalar(bq8, bq8, K ** -0.5, None, ALU.mult))
            dve.wait_ge(pool_const, 6)
            for n in range(HP):
                step_no_wait(nc.vector.tensor_scalar(bv_rows[:, n, :], ones[:, 0:P], bv_c[:, n:n + 1], None, ALU.mult))
            for r in range(4):
                for h in range(2):
                    step_no_wait(nc.vector.tensor_scalar(stack[K:K + 2, r, h, K2, :], ones[K:K + 2, 0:S],
                                                         ident[K:K + 2, K + h:K + h + 1], ROW_SCALE,
                                                         ALU.mult, ALU.mult))
            assert n_step[0] == SMALL_READY, n_step[0]
            dve.wait_ge(act_step, 4)
            for dst, hi_, raw, scale in ((wq_lo, wq_hi, raw_q, K ** -0.5), (wk_lo, wk_hi, raw_k, 1.0),
                                         (wv_lo, wv_hi, raw_v, 1.0), (wo_lo, wo_hi, raw_o, 1.0)):
                step_no_wait(nc.vector.scalar_tensor_tensor(
                    out=dst, in0=raw.rearrange("p (n c) -> p n c", n=HP), scalar=scale, in1=hi_,
                    op0=ALU.mult, op1=ALU.subtract))
            dve.wait_ge(act_step, 6)
            step_no_wait(nc.vector.tensor_tensor(router_lo, ps8[6][:, 0:E], router_hi, ALU.subtract))
            dve.wait_ge(bias_done, 1)
            step_no_wait(nc.vector.tensor_tensor(attn_bias, ps8[7][:, 0:D], bo_b, ALU.add))
            assert n_step[0] == A_DONE, n_step[0]

            def lo_block(n, ready, done):
                dve.wait_ge(ready, n + 1)
                nc.vector.tensor_tensor(xT_lo[:, n * S:(n + 1) * S], ps8[n % 4], xT_hi[:, n * S:(n + 1) * S],
                                        ALU.subtract).then_inc(done, 1)

            for n in range(B):
                lo_block(n, tr_a_hi, tr_a_lo)

            def run(p, u, batch):
                t = p + 3

                def row_max(s, h):
                    pair, q, up = p + 1 + (s + 2) // 4, (s + 2) % 4, u + 1 + (s + 2) // 4
                    if not valid(pair):
                        return
                    dve.wait_ge(max_scores, 8 * pair + 2 * q + h + 1)
                    if q == 0 and h == 0:
                        wait(dve, negmax_done, pair - 1)
                    nc.vector.tensor_reduce(rmax[:, up % 2, q, h:h + 1], ps_max, AX.X, ALU.max).then_inc(max_done, 1)
                    if q == 3 and h == 1:
                        dve.wait_ge(max_done, 8 * pair + 8)
                        wait(dve, maxrow_ps, pair - 1)
                        nc.vector.tensor_scalar(negmax[:, up % 2, :, :], rmax[:, up % 2, :, :], -1.0 / ROW_SCALE,
                                                EXP_SHIFT / ROW_SCALE, ALU.mult, ALU.add).then_inc(negmax_done, 1)

                for s in range(4):
                    if s == 0 and valid(p, -3):
                        _, b = batch_of(u, batch, -3)
                        dve.wait_ge(y_ps, p - 3 + 1)
                        wait(dve, y_added, p - 3)
                        dst = xn[:, bass.ds(b * QT, QT), :] if not isinstance(b, int) else xn[:, b * QT:b * QT + QT, :]
                        nc.vector.tensor_tensor(dst, ps_turn.rearrange("p (t d) -> p t d", t=QT), dst,
                                                ALU.add).then_inc(y_added, 1)
                    row_max(s, 0)
                    if valid(p, -1):
                        dve.wait_ge(ctx_ps, 4 * (p - 1) + s + 1)
                        wait(dve, ctx_done, 4 * (p - 1) + s - 1)
                        nc.vector.reciprocal(rden[:, s % 2, :], ps_ctx[:, K:K + P + 1:P]).then_inc(rden_done, 1)
                    first = p - u % 2
                    if s == 3 and (not isinstance(p, int) or -2 <= first < PAIRS):
                        v, vb = batch_of(u - u % 2, batch, 2)
                        tile, half = vb * (HP // 2) + v // 2, vb * (HP // 4) + v // 4
                        dst = slice(tile, tile + 1) if isinstance(tile, int) else bass.ds(tile, 1)
                        raw = w_raw[:, v // 2 % 2:v // 2 % 2 + 1, :, :]
                        if u % 2 == 0:
                            dve.wait_ge(w_in[v // 2 % 2], (half + 1) * 48)
                            nc.vector.tensor_scalar(w_hi[:, dst, :, :], raw, 1.0, None, ALU.mult).then_inc(w_hi_done, 1)
                        else:
                            dve.wait_ge(w_hi_done, tile + 1)
                            nc.vector.tensor_tensor(w_lo[:, dst, :, :], raw, w_hi[:, dst, :, :],
                                                    ALU.subtract).then_inc(w_split, 1)
                    if s == 1 and valid(p, -2):
                        dve.wait_ge(ctx_hi, p - 2 + 1)
                        nc.vector.tensor_tensor(ctxT_lo[:, u % 2, :], ps_turn, ctxT_hi[:, u % 2, :],
                                                ALU.subtract).then_inc(ctx_lo, 1)
                    row_max(s, 1)
                    if s < 2 and valid(t):
                        n = batch_of(u, batch, 3)[0]
                        dve.wait_ge(qk_hi, 2 * t + s + 1)
                        nc.vector.scalar_tensor_tensor(out=flat[:, (u + 3) % 2, (ZQL, ZKL)[s], :], in0=ps_proj,
                                                       scalar=(bq8, bk_c)[s][:, n:n + 1],
                                                       in1=flat[:, (u + 3) % 2, (ZQH, ZKH)[s], :],
                                                       op0=ALU.add, op1=ALU.subtract).then_inc(qk_lo, 1)
                    if s == 2 and valid(p):
                        dve.wait_ge(v_hi_done, p + 1)
                        nc.vector.tensor_tensor(v_lo[:, u % 2, :, :, :],
                                                ps_proj.rearrange("p (t h c) -> p t h c", t=QT, h=2),
                                                v_hi[:, u % 2, :, :, 0:K], ALU.subtract).then_inc(v_lo_done, 1)

            steps(run, dve)

            def route(m, r, k):
                counted = [ROUTE_AT.get(k, 0)]

                def own(ins):
                    ins.then_inc(route_step, 1)
                    counted[0] += 1

                def settled():
                    dve.wait_ge(route_step, m * ROUTE_STEPS + counted[0])

                def then(ins):
                    own(ins)
                    settled()

                def all_tiles(row):
                    return row.unsqueeze(1).broadcast_to([P, QT, row.shape[1]])

                if k == 4:
                    at = slice(m * QT, (m + 1) * QT) if isinstance(m, int) else bass.ds(m * QT, QT)
                    then(nc.vector.tensor_tensor(ya, xn[:, at, :], all_tiles(attn_bias), ALU.add))
                if k in (5, 10):
                    for t in range(QT):
                        own(nc.vector.bn_stats(bn[:, t, :], (ya if k == 5 else x2[:, r])[:, t, :]))
                    settled()
                if k in (6, 11):
                    for t in range(QT):
                        own(nc.vector.bn_aggr(mean_var[:, t, :], bn[:, t, :]))
                    settled()
                    eps = POST_EPS if k == 6 else LN_EPS
                    nc.vector.tensor_scalar(veps, mean_var[:, :, 1], eps, None, ALU.add).then_inc(c_var, 1)
                if k == 8:
                    for t in range(QT):
                        own(nc.vector.scalar_tensor_tensor(out=ya[:, t, :], in0=ya[:, t, :], scalar=mean_var[:, t, 0:1],
                                                           in1=gamma_b, op0=ALU.subtract, op1=ALU.mult))
                    settled()
                if k == 9:
                    dve.wait_ge(rstd_done, m * 2 + 1)
                    dve.wait_ge(xbeta, m + 1)
                    for t in range(QT):
                        own(nc.vector.scalar_tensor_tensor(out=x2[:, r, t, :], in0=ya[:, t, :], scalar=rstd[:, t:t + 1],
                                                           in1=xin[:, r, t, :], op0=ALU.mult, op1=ALU.add))
                    settled()
                if k == 13:
                    dve.wait_ge(rstd_done, m * 2 + 2)
                    wait(dve, tr_c, m)
                    for t in range(QT):
                        last = nc.vector.tensor_scalar(xf[:, t, :], x2[:, r, t, :], mean_var[:, t, 0:1],
                                                       rstd[:, t:t + 1], ALU.subtract, ALU.mult)
                    last.then_inc(xf_done, 1)
                if k == 17:
                    dve.wait_ge(tr_c_hi, m + 1)
                    nc.vector.tensor_tensor(fT_lo[:, r, :], ps8[7], fT_hi[:, r, :], ALU.subtract).then_inc(tr_c_lo, 1)
                g8 = sfc.rearrange("p t (g e) -> p (t g) e", g=G)
                n4, n2, n1 = QT * G * 4, QT * G * 2, QT * G
                hi4, lo4 = (work1[:, i * n4:(i + 1) * n4].rearrange("p (n e) -> p n e", e=4) for i in range(2))
                hi2, mid2, lo2, sec2 = (work2[:, i * n2:(i + 1) * n2].rearrange("p (n e) -> p n e", e=2) for i in range(4))
                hi1, mid1, lo1, sec1, gsum, rank = (work1[:, i * n1:(i + 1) * n1] for i in range(6))
                if k == 20:
                    dve.wait_ge(sfc_done, m + 1)
                    own(nc.vector.tensor_tensor(hi4, g8[:, :, 0:4], g8[:, :, 4:8], ALU.max))
                    then(nc.vector.tensor_tensor(lo4, g8[:, :, 0:4], g8[:, :, 4:8], ALU.min))
                if k == 21:
                    own(nc.vector.tensor_tensor(hi2, hi4[:, :, 0:2], hi4[:, :, 2:4], ALU.max))
                    own(nc.vector.tensor_tensor(mid2, hi4[:, :, 0:2], hi4[:, :, 2:4], ALU.min))
                    then(nc.vector.tensor_tensor(lo2, lo4[:, :, 0:2], lo4[:, :, 2:4], ALU.max))
                    then(nc.vector.tensor_tensor(sec2, mid2, lo2, ALU.max))
                if k == 22:
                    own(nc.vector.tensor_tensor(hi1, hi2[:, :, 0], hi2[:, :, 1], ALU.max))
                    own(nc.vector.tensor_tensor(mid1, hi2[:, :, 0], hi2[:, :, 1], ALU.min))
                    then(nc.vector.tensor_tensor(lo1, sec2[:, :, 0], sec2[:, :, 1], ALU.max))
                    then(nc.vector.tensor_tensor(sec1, mid1, lo1, ALU.max))
                    then(nc.vector.tensor_tensor(gsum, hi1, sec1, ALU.add))
                mine = gsum.rearrange("p (t g) -> p t g", t=QT).unsqueeze(3).broadcast_to([P, QT, G, G])
                other = gsum.rearrange("p (t g) -> p t g", t=QT).unsqueeze(2).broadcast_to([P, QT, G, G])
                pairs3, pairs4 = (w.rearrange("p (t g h) -> p t g h", t=QT, g=G) for w in (work3, work4))
                taken, masked = (w.rearrange("p (t e) -> p t e", t=QT) for w in (work3, work4))
                if k == 23:
                    own(nc.vector.tensor_tensor(pairs4, other, mine, ALU.is_gt))
                    then(nc.vector.tensor_tensor(pairs3, other, mine, ALU.is_ge))
                if k == 24:
                    then(nc.vector.tensor_tensor(taken, taken, all_tiles(tri), ALU.mult))
                    then(nc.vector.tensor_tensor(work3, work3, work4, ALU.max))
                if k == 25:
                    then(nc.vector.tensor_reduce(rank, work3.rearrange("p (n h) -> p n h", h=G), AX.X, ALU.add))
                    then(nc.vector.tensor_scalar(rank, rank, float(TOPG) - 0.5, None, ALU.is_lt))
                    then(nc.vector.tensor_tensor(work4.rearrange("p (n e) -> p n e", e=EG), g8,
                                                 rank.unsqueeze(2).broadcast_to([P, QT * G, EG]), ALU.mult))
                best = work2[:, 0:QT * TOPK].rearrange("p (t k) -> p t k", t=QT)
                if k == 26:
                    for t in range(QT):
                        own(nc.vector.max(best[:, t, :], masked[:, t, :]))
                    settled()
                if k == 27:
                    for t in range(QT):
                        own(nc.vector.match_replace(taken[:, t, :], best[:, t, :], masked[:, t, :], -3.0e38))
                    settled()
                if k == 28:
                    then(nc.vector.tensor_scalar(work3, work3, -2.0e38, None, ALU.is_lt))
                    then(nc.vector.tensor_tensor(sfc, scores, taken, ALU.mult))
                if k == 29:
                    then(nc.vector.tensor_reduce(total, sfc, AX.X, ALU.add))
                    then(nc.vector.tensor_scalar(total, total, 1e-20, 1 / ROUTE_SCALE, ALU.add, ALU.mult))
                    then(nc.vector.reciprocal(share, total))
                    then(nc.vector.tensor_tensor(sfc, sfc, share.unsqueeze(2).broadcast_to([P, QT, E]), ALU.mult))
                if k == 30:
                    then(nc.vector.tensor_copy(both[:, :, 0, :], sfc))
                    nc.vector.tensor_tensor(both[:, :, 1, :], sfc, both[:, :, 0, :], ALU.subtract).then_inc(coef, 1)
                assert counted[0] == ROUTE_AT.get(k, 0) + ROUTE_COUNT.get(k, 0), k

            def tile(t, r, shared):
                dve.wait_ge(uc_ps, t + 1)
                dve.wait_ge(silu_done, t + 1)
                if not shared:
                    wait(dve, hid_done, t - 1)
                    nc.vector.tensor_tensor(prod[:, r % 2, :], silu_g[:, r % 2, :], ps8[2 + r % 2],
                                            ALU.mult).then_inc(prod_done, 1)
                    dve.wait_ge(prod_done, t + 1)
                wait(dve, hid_lo_done, t - 2)
                if shared:
                    nc.vector.tensor_tensor(hid[:, r % 3, :], silu_g[:, r % 2, :], ps8[2 + r % 2],
                                            ALU.mult).then_inc(hid_done, 1)
                    dve.wait_ge(hid_done, t + 1)
                    nc.vector.tensor_copy(prod[:, r % 2, 0:2], silu_g[:, r % 2, 0:2]).then_inc(prod_done, 1)
                else:
                    nc.vector.tensor_tensor(hid[:, r % 3, :], prod[:, r % 2, :], ps8[4 + r % 2],
                                            ALU.mult).then_inc(hid_done, 1)

            def take_sum(n):
                dve.wait_ge(down_done, (n + 1) * TILES)
                nc.vector.tensor_copy(ysb, ps8[6]).then_inc(y_copied, 1)

            def add_sum(n, r):
                dve.wait_ge(y_back, n + 1)
                nc.vector.tensor_tensor(x2[:, r, :, :], ps8[7].rearrange("p (t d) -> p t d", t=QT), x2[:, r, :, :],
                                        ALU.add).then_inc(out_ready, 1)

            def run_block(n, r, last):
                for k in range(4, TILES if last else TILES + 4):
                    tile(n * TILES + k, (r * TILES + k) % 6, k == TILES)
                    if not last:
                        route(n + 1, 1 - r, k)
                    if k == TILES + 2:
                        take_sum(n)
                    if k == TILES + 3:
                        add_sum(n, r)
                if last:
                    take_sum(n)
                    add_sum(n, r)

            dve.wait_ge(y_added, PAIRS)
            for k in range(TILES):
                route(0, 0, k)
            for t in range(4):
                tile(t, t, t == 0)
            blocks(dve, run_block)

        @block.tensor
        def _(pe):
            def mm(out_, lhsT, rhs, start, stop):
                return nc.tensor.matmul(out_, lhsT, rhs, start=start, stop=stop, skip_group_check=True)

            def product(out_, a_hi, a_lo, b_hi, b_lo, start=True, stop=True):
                mm(out_, a_hi, b_hi, start, False)
                mm(out_, a_hi, b_lo, False, False)
                return mm(out_, a_lo, b_hi, False, stop)

            pe.wait_ge(pool_const, 2)
            pe.wait_ge(in_small, 8 * 16)
            nc.tensor.transpose(ps8[6][:, 0:E], router_raw[0:E, :], ident[0:E, 0:E]).then_inc(router_t, 1)
            pe.wait_ge(in_w, 64)
            pe.wait_ge(dve_step, SMALL_READY)
            for n in range(HP):
                last = mm(ps8[7][:, 0:D], bv_rows[:, n, :], raw_o[:, n * D:(n + 1) * D], n == 0, n == HP - 1)
            last.then_inc(bias_done, 1)

            pe.wait_ge(dve_step, XN_READY)
            for n in range(B):
                if n >= 4:
                    pe.wait_ge(tr_a_lo, n - 3)
                for t in range(QT):
                    last = nc.tensor.transpose(ps8[n % 4][:, t * P:(t + 1) * P], xn[:, n * QT + t, :], ident)
                last.then_inc(tr_a, 1)
            pe.wait_ge(dve_step, A_DONE)
            pe.wait_ge(tr_a_lo, B)
            pe.wait_ge(act_step, 6)

            def tokens(xT, b, off=0, n=S):
                return xT[:, bass.ds(b * S + off, n)] if not isinstance(b, int) else xT[:, b * S + off:b * S + off + n]

            def run(p, u, batch):
                t = p + 3

                def query_tile(s, h):
                    pair, q, up = p + 1 + (s + 2) // 4, (s + 2) % 4, u + 1 + (s + 2) // 4
                    if not valid(pair):
                        return
                    if q == 0 and h == 0:
                        half = (p + 2) // 2 if isinstance(p, int) else batch * (HP // 2) + (u + 2) // 2
                        pe.wait_ge(stacked[up % 2], 96 * (half + 1))
                    wait(pe, max_done, 8 * pair + 2 * q + h)
                    st = stack[:, up % 4, h, :, :]
                    mm(ps_max, st[:, Q1, q * P:(q + 1) * P], st[:, K1, :], True, True).then_inc(max_scores, 1)

                for s in range(4):
                    if valid(p):
                        if s == 0:
                            pe.wait_ge(maxrow, p + 1)
                        wait(pe, exp_done, 4 * p + s - 1)
                        ks = slice(s * P, (s + 1) * P)
                        for h in range(2):
                            o = ps_st[s % 2][:, h * S:(h + 1) * S]
                            st = stack[:, u % 4, h, :, :]
                            mm(o, st[:, K1, ks], st[:, Q1, :], True, False)
                            last = mm(o, st[0:K + 2, K2, ks], st[0:K + 2, Q2, :], False, True)
                        last.then_inc(scores_t, 1)
                    if valid(p, -1):
                        h, q0, o = s // 2, 2 * (s % 2), (u + 1) % 2
                        wait(pe, ctx_done, 4 * (p - 1) + s)
                        if s == 0:
                            pe.wait_ge(v_lo_done, p)
                        for k in range(QT):
                            if s == 0:
                                pe.wait_ge(lo_pool, 4 * (p - 1) + k + 1)
                            for q in range(2):
                                qs = slice((q0 + q) * P, (q0 + q + 1) * P)
                                c = ps_ctx[:, q * P:q * P + K + 1]
                                mm(c, num_hi[:, o, k, h, qs, 1], v_hi[:, o, k, h, :], k == 0 and q == 0, False)
                                mm(c[:, 0:K], num_hi[:, o, k, h, qs, 1], v_lo[:, o, k, h, :], False, False)
                                last = mm(c, num_lo[:, o, k, h, qs], v_hi[:, o, k, h, :], False, k == QT - 1)
                            if k == 0:
                                query_tile(s, 0)
                        last.then_inc(ctx_ps, 1)
                    else:
                        query_tile(s, 0)
                    if s == 2 and valid(p, 1):
                        wait(pe, ctx_lo, p - 2 + 1)
                        if isinstance(p, int):
                            wait(pe, maxrow, p + 1)
                        pe.wait_ge(negmax_done, p + 1 + 1)
                        for k in range(QT):
                            last = mm(ps_turn[K:K + 2, k * P:(k + 1) * P], negmax[:, (u + 1) % 2, k, :], ident16, True, True)
                        last.then_inc(maxrow_ps, 1)
                    if s < 2 and valid(t):
                        n, b = batch_of(u, batch, 3)
                        w_hi, w_lo = ((wq_hi, wq_lo), (wk_hi, wk_lo))[s]
                        if s == 0:
                            wait(pe, v_lo_done, p)
                            if isinstance(t, int):
                                wait(pe, qk_lo, 2 * t)
                        else:
                            pe.wait_ge(qk_lo, 2 * t + 1)
                        product(ps_proj, w_hi[:, n, :], w_lo[:, n, :], tokens(xT_hi, b), tokens(xT_lo, b)).then_inc(qk_proj, 1)
                    if s == 2 and valid(p):
                        n, b = batch_of(u, batch, 0)
                        pe.wait_ge(qk_lo, upto(2 * t + 2, 2 * PAIRS))
                        for k in range(QT):
                            last = product(ps_proj[:, k * P:(k + 1) * P], tokens(xT_hi, b, k * P, P), tokens(xT_lo, b, k * P, P),
                                           wv_hi[:, n, :], wv_lo[:, n, :])
                        last.then_inc(v_proj, 1)
                    if s == 3 and valid(p, -2):
                        n, _ = batch_of(u, batch, -2)
                        pe.wait_ge(ctx_lo, p - 2 + 1)
                        pe.wait_ge(maxrow, upto(p + 1 + 1, PAIRS))
                        for k in range(QT):
                            ks = slice(k * P, (k + 1) * P)
                            last = product(ps_turn[:, ks], ctxT_hi[:, u % 2, ks], ctxT_lo[:, u % 2, ks],
                                           wo_hi[:, n, :], wo_lo[:, n, :])
                        last.then_inc(y_ps, 1)
                    query_tile(s, 1)
                    if s == 0 and valid(p, -2):
                        wait(pe, y_added, p - 2)
                        if isinstance(p, int):
                            wait(pe, maxrow, upto(p + 1, PAIRS))
                        pe.wait_ge(ctx_done, 4 * (p - 2) + 4)
                        for k in range(QT):
                            last = nc.tensor.transpose(ps_turn[:, k * P:(k + 1) * P], ctxn[:, u % 2, k, :], ident)
                        last.then_inc(ctx_t, 1)

            steps(run, pe)

            def route(m, r, k):
                if k == 12:
                    pe.wait_ge(xf_done, m + 1)
                    for t in range(QT):
                        last = nc.tensor.transpose(ps8[7][:, t * P:(t + 1) * P], xf[:, t, :], ident)
                    last.then_inc(tr_c, 1)
                if k == 15:
                    pe.wait_ge(tr_c_lo, m + 1)
                    for t in range(QT):
                        ts_ = slice(t * P, (t + 1) * P)
                        last = product(ps8[7][:, t * E:(t + 1) * E], fT_hi[:, r, ts_], fT_lo[:, r, ts_], router_hi, router_lo)
                    last.then_inc(logits, 1)
                if k == 29:
                    pe.wait_ge(coef, m + 1)
                    for t in range(QT):
                        last = nc.tensor.transpose(ps8[7].bitcast(F16)[:, t * P:(t + 1) * P],
                                                   both[:, t, :, :].rearrange("p k e -> p (k e)"), ident16)
                    last.then_inc(coef_t, 1)

            def gate_up(n, r, k):
                if k >= TILES:
                    n, r, k = n + 1, 1 - r, k - TILES
                t, i = n * TILES + k, r * TILES + k
                wait(pe, silu_done, t - 1)
                product(ps8[i % 2], w_hi[:, k, 0, :], w_lo[:, k, 0, :], fT_hi[:, r, :], fT_lo[:, r, :]).then_inc(g_ps, 1)
                wait(pe, hid_done, t - 1)
                last = product(ps8[2 + i % 2], w_hi[:, k, 1, :], w_lo[:, k, 1, :], fT_hi[:, r, :], fT_lo[:, r, :])
                if k == 1:
                    pe.wait_ge(coef_sb, n + 1)
                if k > 0:
                    last = mm(ps8[4 + i % 2], sel[:, k - 1, :, :].rearrange("p h m -> p (h m)"), coefT[:, r, :], True, True)
                last.then_inc(uc_ps, 1)

            def down(n, r, k):
                if k == TILES:
                    n, r, k = n + 1, 1 - r, 0
                t, i = n * TILES + k, r * TILES + k
                pe.wait_ge(hid_lo_done, t + 1)
                if k == 0:
                    wait(pe, y_copied, n)
                product(ps8[6], w_hi[:, k, 2, :], w_lo[:, k, 2, :], hid_hi[:, i % 3, :], hid_lo[:, i % 3, :],
                        start=k == 0, stop=k == TILES - 1).then_inc(down_done, 1)

            def transpose_sum(n):
                pe.wait_ge(y_copied, n + 1)
                for k in range(QT):
                    last = nc.tensor.transpose(ps8[7][:, k * P:(k + 1) * P], ysb[:, k * P:(k + 1) * P], ident)
                last.then_inc(y_back, 1)

            def run_block(n, r, last):
                for k in range(1, TILES if last else TILES + 1):
                    if not (last and k + 3 >= TILES):
                        gate_up(n, r, k + 3)
                    down(n, r, k)
                    if not last:
                        route(n + 1, 1 - r, k)
                transpose_sum(n)

            for k in range(TILES):
                route(0, 0, k)
            pe.wait_ge(w_split, TILES)
            pe.wait_ge(sel_done, 3)
            for k in range(4):
                gate_up(0, 0, k)
            down(0, 0, 0)
            blocks(pe, run_block)


_VAR = NT + 7
A_VAR = _VAR
XN_READY = A_VAR + NT
SMALL_READY = XN_READY + 1 + HP + 8
A_DONE = SMALL_READY + 6

ROUTE_COUNT = {4: 1, 5: QT, 6: QT, 8: QT, 9: QT, 10: QT, 11: QT, 20: 2, 21: 4, 22: 5, 23: 2, 24: 2, 25: 3,
               26: QT, 27: QT, 28: 2, 29: 4, 30: 1}
ROUTE_AT = {k: sum(c for j, c in ROUTE_COUNT.items() if j < k) for k in ROUTE_COUNT}
ROUTE_STEPS = sum(ROUTE_COUNT.values())


_INS = ["x", "Wq", "bq", "Wk", "bk", "Wv", "bv", "Wo", "bo", "gamma", "beta"]
_FFN = ["router_w", "e_bias", "Wg", "Wu", "Wd", "SWg", "SWu", "SWd"]


def kernel(**inputs):
    import numpy as np
    import concourse.bacc as bacc
    from concourse.bass_utils import run_bass_kernel_spmd

    nc = bacc.Bacc("TRN2", target_bir_lowering=False, num_devices=1)
    arrays, args = {}, []
    for name in ["L0_attn_" + n for n in _INS] + ["L0_ffn_" + n for n in _FFN]:
        a = np.ascontiguousarray(inputs[name])
        arrays[f"in_{name}"] = a
        args.append(nc.dram_tensor(f"in_{name}", a.shape, mybir.dt.from_np(a.dtype), kind="ExternalInput").ap())
    out = nc.dram_tensor("out_0", (B, S, D), F32, kind="ExternalOutput").ap()
    layer(nc, *args, out)
    result = run_bass_kernel_spmd(nc, [arrays], core_ids=[0])
    return result.results[0]["out_0"]
```

```python
from contextlib import ExitStack

import concourse.bass as bass
from concourse import mybir

P = 128
F32 = mybir.dt.float32
F16 = mybir.dt.float16
BF16 = mybir.dt.bfloat16
ALU = mybir.AluOpType
ACT = mybir.ActivationFunctionType
AX = mybir.AxisListType

B, S, D = 8, 512, 128
H, K = 16, 64
HP = H // 2
PAIRS = B * HP
QT = S // P
TOK = B * S
NT = TOK // P
E, G, TOPG, TOPK = 64, 8, 4, 8
EG = E // G
EP = E // 2
TILES = EP + 1
ROUTE_SCALE = 2.5
LN_EPS, POST_EPS = 1e-5, 1e-3
ROW_SCALE = 1024.0
EXP_SHIFT = 5.0
Q1, Q2, K1, K2 = range(4)
ZQH, ZQL, ZKH, ZKL = range(4)
UNROLL = HP
FIRST, LAST = 4, 60


def layer(nc, x, Wq, bq, Wk, bk, Wv, bv, Wo, bo, gamma, beta, router_w, e_bias,
          Wg, Wu, Wd, SWg, SWu, SWd, out):
    with ExitStack() as ctx:
        def sem(name):
            return ctx.enter_context(nc.semaphore(name))

        ARENA = 53120
        arena = ctx.enter_context(nc.sbuf_tensor("arena", [P, ARENA], F32))
        top = [0]

        def take(words, at=None):
            if at is None:
                at = top[0]
                top[0] += words
                assert top[0] <= ARENA, top[0]
            return arena[:, at:at + words]

        def f16(ap):
            return ap.bitcast(F16)

        xn = take(NT * D).rearrange("p (t d) -> p t d", t=NT)
        xT_hi_at, xT_lo_at = top[0], top[0] + TOK // 2
        xT_hi = f16(take(TOK // 2))
        xT_lo = f16(take(TOK // 2))
        ident = take(P)
        ident16 = f16(take(P // 2))
        gamma_b, beta_b, attn_bias = take(D), take(D), take(D)
        ebias_b = take(E)
        router_hi, router_lo = f16(take(E // 2)), f16(take(E // 2))
        bq8, bk_c, bv_c = take(HP), take(HP), take(HP)
        half_pow = take(QT)
        w_hi, w_lo = (f16(take(TILES * 3 * P // 2)).rearrange("p (t k n) -> p t k n", t=TILES, k=3) for _ in range(2))
        wqkv_at = top[0]
        wq_hi, wq_lo, wk_hi, wk_lo, wv_hi, wv_lo = (
            f16(take(H * K // 2)).rearrange("p (n c) -> p n c", n=HP) for _ in range(6))
        wo_hi, wo_lo = (f16(take(HP * D // 2)).rearrange("p (n c) -> p n c", n=HP) for _ in range(2))
        stack_at = top[0]
        stack = f16(take(4 * 2 * 4 * S // 2)).rearrange("p (r h k q) -> p r h k q", r=4, h=2, k=4)
        flat = f16(take(2 * 4 * S // 2)).rearrange("p (r k q) -> p r k q", r=2, k=4)
        v_hi = f16(take(2 * QT * 2 * (K + 1) // 2)).rearrange("p (r t h c) -> p r t h c", r=2, t=QT, h=2)
        v_lo = f16(take(2 * QT * 2 * K // 2)).rearrange("p (r t h c) -> p r t h c", r=2, t=QT, h=2)
        num_at = top[0]
        num_flat = take(2 * QT * 2 * S)
        num = num_flat.rearrange("p (r t h q) -> p r t h q", r=2, t=QT, h=2)
        num_hi = num_flat.bitcast(BF16).rearrange("p (r t h q w) -> p r t h q w", r=2, t=QT, h=2, w=2)
        numlo_at = top[0]
        num_lo = f16(take(2 * QT * 2 * S // 2)).rearrange("p (r t h q) -> p r t h q", r=2, t=QT, h=2)
        ctxn = take(2 * QT * P).rearrange("p (r t c) -> p r t c", r=2, t=QT)
        ctxT_hi = f16(take(2 * S // 2)).rearrange("p (r q) -> p r q", r=2)
        ctxT_lo = f16(take(2 * S // 2)).rearrange("p (r q) -> p r q", r=2)
        rmax = take(2 * QT * 2).rearrange("p (r t h) -> p r t h", r=2, t=QT)
        negmax = f16(take(2 * QT)).rearrange("p (r t h) -> p r t h", r=2, t=QT)
        rden = take(2 * 2).rearrange("p (r t) -> p r t", r=2)
        xT_of = [[f16(take(S // 2)) for _ in range(2)] for _ in range(2)]
        w_raw = take(2 * 3 * P).rearrange("p (r k n) -> p r k n", r=2, k=3)
        raw_q, raw_k, raw_v, raw_o = (take(H * K, num_at + i * H * K) for i in range(4))
        bv_rows = take(HP * P, num_at + 4 * H * K).rearrange("p (n c) -> p n c", n=HP)
        router_raw = take(D, num_at + 5 * H * K)
        bo_b = take(D, num_at + 5 * H * K + D)
        row_scale = take(S, num_at + 5 * H * K + 2 * D)
        stat = take(8 * NT, num_at + 5 * H * K + 2 * D + S).rearrange("p (k t) -> p k t", k=8)
        half_pow_a = take(NT, num_at + 5 * H * K + 2 * D + S + 8 * NT)
        def tiles4(ap):
            return ap.rearrange("p (t d) -> p t d", t=QT)

        dead = (B - 1) * S // 2
        top[0] = xT_hi_at
        xin, x2 = [tiles4(take(S))], [tiles4(take(S))]
        ya = tiles4(take(S))
        bn, mean_var = tiles4(take(QT * 6)), tiles4(take(QT * 2))
        veps, rstd, total, share = (take(QT) for _ in range(4))
        tri = take(G * G)
        assert top[0] <= xT_hi_at + dead
        top[0] = xT_lo_at
        xf = tiles4(take(S))
        fT_hi, fT_lo = ([f16(take(S // 2))] for _ in range(2))
        coefT = [take(S)[0:E, :]]
        scores = tiles4(take(QT * E))
        assert top[0] <= xT_lo_at + dead
        top[0] = wqkv_at
        work1, work2, work3, work4 = (take(QT * E) for _ in range(4))
        sfc = tiles4(take(QT * E))
        assert top[0] <= wqkv_at + 4 * (H * K // 2)
        top[0] = stack_at
        xin.append(tiles4(take(S)))
        x2.append(tiles4(take(S)))
        for ring in (fT_hi, fT_lo):
            ring.append(f16(take(S // 2)))
        coefT.append(take(S)[0:E, :])
        coef_b = take(4 * S).rearrange("p (r q) -> p r q", r=4)
        silu_g = take(3 * S).rearrange("p (r q) -> p r q", r=3)
        prod = take(2 * S).rearrange("p (r q) -> p r q", r=2)
        hid = take(6 * S).rearrange("p (r q) -> p r q", r=6)
        hid_hi, hid_lo = (f16(take(6 * S // 2)).rearrange("p (r q) -> p r q", r=6) for _ in range(2))
        ysb = take(S)

        bank = [ctx.enter_context(nc.psum_tensor(f"bank{i}", [P, 1024], F32)) for i in range(4)]
        ps_st = [bank[0], bank[1]]
        ps8 = [bank[i // 2][:, (i % 2) * 512:(i % 2) * 512 + 512] for i in range(8)]
        ps_max = ps8[4]
        ps_ctx = ps8[5]
        ps_proj = ps8[6]
        ps_turn = ps8[7]

        in_x0 = sem("in_x0")
        in_x = sem("in_x")
        in_qk = sem("in_qk")
        in_rest = sem("in_rest")
        w_in = [sem("w_in0"), sem("w_in1")]
        w_hi_done = sem("w_hi_done")
        w_split = sem("w_split")
        dve_step = sem("dve_step")
        act_step = sem("act_step")
        bv_spread = sem("bv_spread")
        a_norm = sem("a_norm")
        a_norm_pool = sem("a_norm_pool")
        pool_const = sem("pool_const")
        tr_a = sem("tr_a")
        tr_a_hi = sem("tr_a_hi")
        tr_a_lo = sem("tr_a_lo")
        bias_done = sem("bias_done")
        router_t = sem("router_t")
        a_rstd = sem("a_rstd")
        x_of = [sem("x_of0"), sem("x_of1")]
        qk_proj = sem("qk_proj")
        qk_hi = sem("qk_hi")
        qk_lo = sem("qk_lo")
        v_proj = sem("v_proj")
        v_hi_done = sem("v_hi_done")
        v_lo_done = sem("v_lo_done")
        stacked = [sem("stacked0"), sem("stacked1")]
        max_scores = sem("max_scores")
        max_done = sem("max_done")
        negmax_done = sem("negmax_done")
        maxrow_ps = sem("maxrow_ps")
        maxrow = sem("maxrow")
        scores_t = sem("scores_t")
        exp_done = sem("exp_done")
        lo_pool = sem("lo_pool")
        ctx_ps = sem("ctx_ps")
        rden_done = sem("rden_done")
        ctx_done = sem("ctx_done")
        ctx_t = sem("ctx_t")
        ctx_hi = sem("ctx_hi")
        ctx_lo = sem("ctx_lo")
        y_ps = sem("y_ps")
        y_added = sem("y_added")
        x_in = [sem("x_in0"), sem("x_in1")]
        xbeta = sem("xbeta")
        rstd_done = sem("rstd_done")
        c_var = sem("c_var")
        xf_done = sem("xf_done")
        tr_c = sem("tr_c")
        tr_c_hi = sem("tr_c_hi")
        tr_c_lo = sem("tr_c_lo")
        logits = sem("logits")
        sigm = sem("sigm")
        coef = sem("coef")
        sfc_done = sem("sfc_done")
        coef_t = sem("coef_t")
        coef_sb = sem("coef_sb")
        route_step = sem("route_step")
        coef_in = [sem(f"coef_in{i}") for i in range(4)]
        tri_done = sem("tri_done")
        g_ps = sem("g_ps")
        u_ps = sem("u_ps")
        silu_done = sem("silu_done")
        prod_done = sem("prod_done")
        hid_done = sem("hid_done")
        hid_hi_done = sem("hid_hi_done")
        hid_lo_done = sem("hid_lo_done")
        down_done = sem("down_done")
        y_copied = sem("y_copied")
        y_back = sem("y_back")
        out_ready = sem("out_ready")
        out_sent = sem("out_sent")

        def bank_c(m):
            return ps_max if isinstance(m, int) and m == 0 else ps_turn

        def block_0_at(p, s):
            if not isinstance(p, int) or p < LAST:
                return range(0)
            slot = (p - LAST) * 4 + s
            return range(slot + 1, slot + 2) if slot < 16 else range(slot * 3 - 31, min(slot * 3 - 28, C_PARTS))

        def wait(eng, s, value):
            if isinstance(value, int) and value <= 0:
                return
            eng.wait_ge(s, value)

        def upto(value, most):
            return min(value, most) if isinstance(value, int) else value

        def valid(pair, off=0):
            return not isinstance(pair, int) or 0 <= pair + off < PAIRS

        def steps(run, eng):
            for p in range(-3, FIRST):
                run(p, p % UNROLL, p // HP)
            with eng.Fori(0, (LAST - FIRST) // UNROLL) as i:
                for u in range(UNROLL):
                    run(i * UNROLL + (FIRST + u), (FIRST + u) % UNROLL, i + (FIRST + u) // HP)
            for p in range(LAST, PAIRS + 3):
                run(p, p % UNROLL, p // HP)

        def batch_of(u, batch, off):
            return (u + off) % HP, batch + (u + off) // HP

        def blocks(eng, run):
            run(0, 0, False)
            with eng.Fori(0, B // 2 - 1) as i:
                run(i * 2 + 1, 1, False)
                run(i * 2 + 2, 0, False)
            run(B - 1, 1, True)

        block = ctx.enter_context(nc.Block())

        @block.sync
        def _(sp):
            xv = x.rearrange("b (t p) d -> p (b t) d", p=P)
            def vector(dst, src, done):
                with nc.allow_non_contiguous_dma(reason="small vectors"):
                    sp.dma_start(dst, src.rearrange("h k -> (h k)").rearrange("(n p) -> p n", p=P)).then_inc(done, 16)

            sp.dma_start(xn[:, 0:QT, :], xv[:, 0:QT, :]).then_inc(in_x0, 16)
            sp.dma_start(raw_q, Wq.rearrange("d h k -> d (h k)")).then_inc(in_qk, 16)
            sp.dma_start(raw_k, Wk.rearrange("d h k -> d (h k)")).then_inc(in_qk, 16)
            vector(bq8, bq, in_qk)
            vector(bk_c, bk, in_qk)
            sp.dma_start(xn[:, QT:, :], xv[:, QT:, :]).then_inc(in_x, 16)
            sp.dma_start(raw_v, Wv.rearrange("d h k -> d (h k)")).then_inc(in_rest, 16)
            sp.dma_start(raw_o.rearrange("p (n c) -> p n c", n=HP),
                         Wo.rearrange("h k d -> (h k) d").rearrange("(n p) d -> p n d", p=P)).then_inc(in_rest, 16)
            vector(bv_c, bv, in_rest)
            for dst, src in ((gamma_b, gamma), (beta_b, beta), (bo_b, bo), (ebias_b, e_bias)):
                sp.dma_start(dst, src.partition_broadcast(P)).then_inc(in_rest, 16)
            sp.dma_start(router_raw[0:E, :], router_w).then_inc(in_rest, 16)
            for n, src in enumerate((SWg, SWu, SWd)):
                sp.dma_start(w_raw[:, 0, n, :], src).then_inc(w_in[0], 16)

            def run(p, u, batch):
                t = p + 3
                if valid(t):
                    wait(sp, scores_t, 4 * p)
                    if u % 4 == 0 and (not isinstance(p, int) or p == 0):
                        half, b = (1, batch) if u == 0 else (0, batch + 1)
                        if isinstance(p, int):
                            sp.wait_ge(tr_a_lo, 1)
                        else:
                            sp.wait_ge(v_proj, p)
                        for dst, src in zip(xT_of[half], (xT_hi, xT_lo)):
                            src = src[:, b * S:(b + 1) * S] if isinstance(b, int) else src[:, bass.ds(b * S, S)]
                            sp.dma_start(dst, src).then_inc(x_of[half], 16)
                    r, z, odd = (u + 3) % 4, (u + 3) % 2, (u + 3) % 2
                    sp.wait_ge(qk_lo, 2 * t + 2)
                    for h in range(2):
                        a = flat[h * K:(h + 1) * K, z, :, :]
                        high, low = stack[0:K, r, h, :, :], stack[K:P, r, h, :, :]
                        sp.dma_start(high[:, Q1:Q2 + 1, :], a[:, ZQH:ZQH + 1, :].broadcast_to([K, 2, S])).then_inc(stacked[odd], 16)
                        sp.dma_start(high[:, K1:K2 + 1, :], a[:, ZKH:ZKL + 1, :]).then_inc(stacked[odd], 16)
                        sp.dma_start(low[:, Q1:K1 + 1:2, :], a[:, ZQL:ZKH + 1, :]).then_inc(stacked[odd], 16)

                w = p + 2
                if u % 2 == 0 and (not isinstance(w, int) or 0 <= w < PAIRS):
                    v, vb = batch_of(u, batch, 2)
                    tile, r = vb * (HP // 2) + v // 2 + 1, (v // 2 + 1) % 2
                    wait(sp, w_split, tile - 1)
                    j = tile - 1
                    e2 = slice(2 * j, 2 * j + 2) if isinstance(j, int) else bass.ds(j * 2, 2)
                    for n, src in enumerate((Wg, Wu)):
                        sp.dma_start(w_raw[:, r, n, :].rearrange("p (e i) -> p e i", e=2),
                                     src[e2].rearrange("e h i -> h e i")).then_inc(w_in[r], 16)
                    sp.dma_start(w_raw[:, r, 2, :], Wd[e2].rearrange("e i h -> (e i) h")).then_inc(w_in[r], 16)

            steps(run, sp)

            xv = x.rearrange("b (t p) d -> b p t d", p=P)
            ov = out.rearrange("b (t p) d -> b p t d", p=P)

            def rows(n):
                return slice(n, n + 1) if isinstance(n, int) else bass.ds(n, 1)

            def load_x(m, r):
                sp.dma_start(xin[r], xv[rows(m)].rearrange("o p t d -> p (o t) d")).then_inc(x_in[r], 16)

            def send(n, r):
                sp.wait_ge(out_ready, n + 1)
                sp.dma_start(ov[rows(n)].rearrange("o p t d -> p (o t) d"), x2[r]).then_inc(out_sent, 16)

            def run_block(n, r, last):
                for k in range(1, TILES):
                    if k == 1:
                        sp.wait_ge(coef_sb, n + 1)
                    if k > 4 or not isinstance(n, int) or n > 0:
                        sp.wait_ge(hid_done, n * TILES + (k - 4 + 1 if k > 4 else k - 5 + 1))
                    sp.dma_start(coef_b[:, (k - 1) % 4, :],
                                 coefT[r][2 * k - 2:2 * k, :].unsqueeze(1).broadcast_to([2, E, S])).then_inc(coef_in[(k - 1) % 4], 16)
                    if k == 1 and not last:
                        load_x(n + 1, 1 - r)
                    if k == 7 and (not isinstance(n, int) or n > 0):
                        send(n - 1, 1 - r)

            sp.wait_ge(scores_t, 4 * LAST)
            load_x(0, 0)
            blocks(sp, run_block)
            send(B - 1, (B - 1) % 2)
            sp.wait_ge(out_sent, 16 * B)

        @block.gpsimd
        def _(pool):
            pool.memset(ident, 0.0).then_inc(pool_const, 1)
            pool.wait_ge(pool_const, 1)
            pool.affine_select(out=ident, in_=ident, compare_op=ALU.not_equal, fill=1.0, base=0,
                               pattern=[[-1, P]], channel_multiplier=1).then_inc(pool_const, 1)
            pool.memset(row_scale, ROW_SCALE).then_inc(pool_const, 1)
            pool.memset(v_hi[:, :, :, :, K:K + 1], 1.0).then_inc(pool_const, 1)
            pool.memset(half_pow, -0.5).then_inc(pool_const, 1)
            pool.memset(half_pow_a, -0.5).then_inc(pool_const, 1)
            pool.wait_ge(pool_const, 6)
            def deviations(tiles, counted):
                pool.wait_ge(dve_step, counted)
                pool.tensor_tensor(stat[:, 1, tiles], stat[:, 6, tiles], half_pow_a[:, tiles], ALU.pow).then_inc(a_rstd, 1)

            deviations(slice(0, QT), A_VAR0)
            pool.wait_ge(in_rest, 8 * 16)
            for n in range(HP):
                pool.tensor_copy(bv_rows[:, n, :], bv_c[:, n:n + 1].broadcast_to([P, P])).then_inc(bv_spread, 1)
            deviations(slice(QT, NT), A_VAR1)
            pool.wait_ge(a_rstd, 2)
            for n in range(NORM_POOL, B):
                for t in range(n * QT, (n + 1) * QT):
                    last = pool.tensor_scalar(xn[:, t, :], xn[:, t, :], stat[:, 0, t:t + 1], stat[:, 1, t:t + 1],
                                              ALU.subtract, ALU.mult)
                last.then_inc(a_norm_pool, 1)

            def route(m, r, k):
                if k == 1 and isinstance(m, int) and m == 0:
                    pool.wait_ge(scores_t, 4 * LAST)
                    pool.memset(tri, 1.0).then_inc(tri_done, 1)
                    pool.wait_ge(tri_done, 1)
                    pool.affine_select(out=tri.rearrange("p (g h) -> p g h", g=G), in_=tri.rearrange("p (g h) -> p g h", g=G),
                                       compare_op=ALU.is_gt, fill=0.0, base=0, pattern=[[1, G], [-1, G]],
                                       channel_multiplier=0).then_inc(tri_done, 1)
                if k in (3, 8):
                    pool.wait_ge(c_var, m * 2 + (1 if k == 3 else 2))
                    pool.tensor_tensor(rstd, veps, half_pow, ALU.pow).then_inc(rstd_done, 1)
                if k == 14:
                    pool.wait_ge(sigm, m + 1)
                    pool.tensor_tensor(sfc, scores, ebias_b.unsqueeze(1).broadcast_to([P, QT, E]),
                                       ALU.add).then_inc(sfc_done, 1)
                if k == 2:
                    count = m // 2 + 1 if isinstance(m, int) else block_i[0] + 2
                    pool.wait_ge(x_in[r], count * 16)
                    pool.tensor_tensor(xin[r], xin[r],
                                       beta_b.unsqueeze(1).broadcast_to([P, QT, D]), ALU.add).then_inc(xbeta, 1)

            def run(p, u, batch):
                def lo(s):
                    pool.wait_ge(exp_done, 4 * p + s + 1)
                    if s == 0:
                        wait(pool, ctx_ps, 4 * (p - 2) + 4)
                    pool.tensor_tensor(num_lo[:, u % 2, s, :, :], num[:, u % 2, s, :, :],
                                       num_hi[:, u % 2, s, :, :, 1], ALU.subtract).then_inc(lo_pool, 1)

                if valid(p):
                    for s in range(4):
                        lo(s)
                for s in range(4):
                    for k in block_0_at(p, s):
                        route(0, 0, k)

            steps(run, pool)

            def tile(t, r):
                pool.wait_ge(hid_hi_done, t + 1)
                wait(pool, down_done, t - 5)
                pool.tensor_tensor(hid_lo[:, r, :], hid[:, r, :], hid_hi[:, r, :],
                                   ALU.subtract).then_inc(hid_lo_done, 1)

            block_i = [None]

            def run_block(n, r, last):
                for k in range(1, TILES if last else TILES + 1):
                    tile(n * TILES + k, (r * TILES + k) % 6)
                    if not last:
                        route(n + 1, 1 - r, k)

            tile(0, 0)
            run_block(0, 0, False)
            with pool.Fori(0, B // 2 - 1) as i:
                block_i[0] = i
                run_block(i * 2 + 1, 1, False)
                run_block(i * 2 + 2, 0, False)
            run_block(B - 1, 1, True)

        @block.scalar
        def _(act):
            n_act = [0]

            def step(ins):
                ins.then_inc(act_step, 1)
                n_act[0] += 1

            act.wait_ge(pool_const, 3)
            step(nc.scalar.activation(ident16, ident, ACT.Copy))
            for r in range(4):
                for h in range(2):
                    step(nc.scalar.activation(stack[K:K + 2, r, h, K2, :], row_scale[K:K + 2, :], ACT.Copy,
                                              scale=ident[K:K + 2, K + h:K + h + 1]))
            act.wait_ge(in_qk, 4 * 16)
            step(nc.scalar.activation(wq_hi, raw_q.rearrange("p (n c) -> p n c", n=HP), ACT.Copy, scale=K ** -0.5))
            step(nc.scalar.activation(wk_hi, raw_k.rearrange("p (n c) -> p n c", n=HP), ACT.Copy))
            assert n_act[0] == ACT_QK

            def hi_block(n):
                act.wait_ge(tr_a, n + 1)
                nc.scalar.activation(xT_hi[:, n * S:(n + 1) * S], ps8[n % 4], ACT.Copy).then_inc(tr_a_hi, 1)

            def rest_of_a(p, s):
                if (p, s) == (-2, 2):
                    act.wait_ge(in_rest, 8 * 16)
                    step(nc.scalar.activation(wv_hi, raw_v.rearrange("p (n c) -> p n c", n=HP), ACT.Copy))
                    step(nc.scalar.activation(wo_hi, raw_o.rearrange("p (n c) -> p n c", n=HP), ACT.Copy))
                    act.wait_ge(router_t, 1)
                    step(nc.scalar.activation(router_hi, ps8[5][:, 0:E], ACT.Copy))
                    assert n_act[0] == ACT_REST
                if (p, s) in TURN_AT:
                    for n in TURN_AT[p, s]:
                        hi_block(n)

            hi_block(0)

            def route(m, r, k):
                if k == 11:
                    act.wait_ge(tr_c, m + 1)
                    nc.scalar.activation(fT_hi[r], bank_c(m), ACT.Copy).then_inc(tr_c_hi, 1)
                if k == 14:
                    act.wait_ge(logits, m + 1)
                    nc.scalar.activation(scores, bank_c(m)[:, 0:QT * E].rearrange("p (t e) -> p t e", t=QT), ACT.Sigmoid).then_inc(sigm, 1)
                if k == 30:
                    act.wait_ge(coef_t, m + 1)
                    nc.scalar.activation(coefT[r], bank_c(m)[0:E, :], ACT.Copy).then_inc(coef_sb, 1)

            def run(p, u, batch):
                t = p + 3

                def hi(which, n):
                    act.wait_ge(qk_proj, 2 * t + which + 1)
                    if which == 0 and (not isinstance(t, int) or t >= 2):
                        act.wait_ge(max_scores, 8 * (t - 2) + 1)
                    bias = (bq8, bk_c)[which]
                    nc.scalar.activation(flat[:, (u + 3) % 2, (ZQH, ZKH)[which], :], ps_proj, ACT.Identity,
                                         bias=bias[:, n:n + 1]).then_inc(qk_hi, 1)

                for s in range(4):
                    if valid(p):
                        act.wait_ge(scores_t, 4 * p + s + 1)
                        if s == 0:
                            wait(act, ctx_ps, 4 * (p - 2) + 4)
                        if isinstance(p, int) and p == 0 and s == 0:
                            act.wait_ge(dve_step, A_DONE)
                        nc.scalar.activation(num[:, u % 2, s, :, :],
                                             ps_st[s % 2][:, :].rearrange("p (h q) -> p h q", h=2),
                                             ACT.Exp).then_inc(exp_done, 1)
                    if s == 2 and valid(p, 1):
                        act.wait_ge(maxrow_ps, p + 1 + 1)
                        nc.scalar.activation(stack[K:K + 2, (u + 1) % 4, :, Q2, :],
                                             ps_turn[K:K + 2, :].unsqueeze(1).broadcast_to([2, 2, S]),
                                             ACT.Copy).then_inc(maxrow, 1)
                    if valid(p, -1):
                        h, q0 = s // 2, 2 * (s % 2)
                        act.wait_ge(rden_done, 4 * (p - 1) + s + 1)
                        if s == 0:
                            wait(act, ctx_t, p - 3 + 1)
                        for q in range(2):
                            last = nc.scalar.activation(ctxn[:, (u + 1) % 2, q0 + q, h * K:(h + 1) * K],
                                                        ps_ctx[:, q * P:q * P + K], ACT.Copy,
                                                        scale=rden[:, s % 2, q:q + 1])
                        last.then_inc(ctx_done, 1)
                    if s == 0 and valid(t):
                        hi(0, batch_of(u, batch, 3)[0])
                    if s == 1 and valid(t):
                        hi(1, batch_of(u, batch, 3)[0])
                    if s == 2 and valid(p):
                        act.wait_ge(v_proj, p + 1)
                        wait(act, ctx_ps, 4 * (p - 2) + 4)
                        nc.scalar.activation(v_hi[:, u % 2, :, :, 0:K],
                                             ps_proj.rearrange("p (t h c) -> p t h c", t=QT, h=2),
                                             ACT.Copy).then_inc(v_hi_done, 1)
                    if s == 0 and valid(p, -2):
                        act.wait_ge(ctx_t, p - 2 + 1)
                        wait(act, y_ps, p - 4 + 1)
                        nc.scalar.activation(ctxT_hi[:, u % 2, :], ps_turn, ACT.Copy).then_inc(ctx_hi, 1)
                    if isinstance(p, int) and p < 0:
                        rest_of_a(p, s)
                    for k in block_0_at(p, s):
                        route(0, 0, k)

            steps(run, act)

            def silu(t, r):
                act.wait_ge(g_ps, t + 1)
                wait(act, prod_done, t - 2)
                nc.scalar.activation(silu_g[:, r % 3, :], ps8[r % 3], ACT.Silu).then_inc(silu_done, 1)

            def hid_hi_tile(t, r):
                act.wait_ge(hid_done, t + 1)
                wait(act, down_done, t - 5)
                nc.scalar.activation(hid_hi[:, r, :], hid[:, r, :], ACT.Copy).then_inc(hid_hi_done, 1)

            def take_sum(n):
                act.wait_ge(down_done, (n + 1) * TILES)
                nc.scalar.activation(ysb, ps8[6], ACT.Copy).then_inc(y_copied, 1)

            def run_block(n, r, last):
                for k in range(1, TILES if last else TILES + 1):
                    silu(n * TILES + k, (r * TILES + k) % 6)
                    hid_hi_tile(n * TILES + (k - 1), (r * TILES + k - 1) % 6)
                    if k == 2 and (not isinstance(n, int) or n > 0):
                        take_sum(n - 1)
                    if not last:
                        route(n + 1, 1 - r, k)
                if last:
                    hid_hi_tile(n * TILES + (TILES - 1), (r * TILES + TILES - 1) % 6)

            silu(0, 0)
            blocks(act, run_block)
            take_sum(B - 1)

        @block.vector
        def _(dve):
            n_step = [0]

            def step(ins):
                ins.then_inc(dve_step, 1)
                n_step[0] += 1
                dve.wait_ge(dve_step, n_step[0])

            def step_no_wait(ins):
                ins.then_inc(dve_step, 1)
                n_step[0] += 1

            stats_a = take(NT * 6, numlo_at).rearrange("p (t k) -> p t k", k=6)

            def statistics(t0, t1):
                for t in range(t0, t1):
                    step_no_wait(nc.vector.bn_stats(stats_a[:, t, :], xn[:, t, :]))

            def variance(t0, t1, expected):
                dve.wait_ge(dve_step, n_step[0])
                m0, m1, c0, c1 = (stats_a[:, t0:t1, i] for i in (1, 4, 2, 5))
                st = stat[:, :, t0:t1]
                step_no_wait(nc.vector.tensor_tensor(st[:, 2, :], m0, m1, ALU.add))
                step_no_wait(nc.vector.tensor_tensor(st[:, 3, :], m0, m1, ALU.subtract))
                step(nc.vector.tensor_tensor(st[:, 4, :], c0, c1, ALU.add))
                step_no_wait(nc.vector.tensor_scalar(st[:, 0, :], st[:, 2, :], 0.5, None, ALU.mult))
                step(nc.vector.scalar_tensor_tensor(out=st[:, 5, :], in0=st[:, 3, :], scalar=0.25,
                                                    in1=st[:, 3, :], op0=ALU.mult, op1=ALU.mult))
                step(nc.vector.scalar_tensor_tensor(out=st[:, 2, :], in0=st[:, 4, :], scalar=1.0 / D,
                                                    in1=st[:, 5, :], op0=ALU.mult, op1=ALU.add))
                step(nc.vector.tensor_scalar(st[:, 6, :], st[:, 2, :], LN_EPS, None, ALU.add))
                assert n_step[0] == expected, (n_step[0], expected)

            dve.wait_ge(in_x0, 16)
            statistics(0, QT)
            variance(0, QT, A_VAR0)
            dve.wait_ge(a_rstd, 1)
            for t in range(QT):
                step_no_wait(nc.vector.tensor_scalar(xn[:, t, :], xn[:, t, :], stat[:, 0, t:t + 1],
                                                     stat[:, 1, t:t + 1], ALU.subtract, ALU.mult))
            assert n_step[0] == XN_READY, n_step[0]
            dve.wait_ge(in_qk, 4 * 16)
            step_no_wait(nc.vector.tensor_scalar(bq8, bq8, K ** -0.5, None, ALU.mult))

            def weights_lo(dst, hi_, raw, scale=1.0):
                step_no_wait(nc.vector.scalar_tensor_tensor(
                    out=dst, in0=raw.rearrange("p (n c) -> p n c", n=HP), scalar=scale, in1=hi_,
                    op0=ALU.mult, op1=ALU.subtract))

            dve.wait_ge(act_step, ACT_QK)
            weights_lo(wq_lo, wq_hi, raw_q, K ** -0.5)
            weights_lo(wk_lo, wk_hi, raw_k)
            assert n_step[0] == QK_READY, n_step[0]

            def lo_block(n):
                dve.wait_ge(tr_a_hi, n + 1)
                nc.vector.tensor_tensor(xT_lo[:, n * S:(n + 1) * S], ps8[n % 4], xT_hi[:, n * S:(n + 1) * S],
                                        ALU.subtract).then_inc(tr_a_lo, 1)

            def rest_of_a(p, s):
                if (p, s) in STATS_AT:
                    dve.wait_ge(in_x, 16)
                    statistics(*STATS_AT[p, s])
                if (p, s) == (-2, 1):
                    variance(QT, NT, A_VAR1)
                if (p, s) == (-2, 3):
                    dve.wait_ge(act_step, ACT_REST)
                    weights_lo(wv_lo, wv_hi, raw_v)
                    weights_lo(wo_lo, wo_hi, raw_o)
                    step_no_wait(nc.vector.tensor_tensor(router_lo, ps8[5][:, 0:E], router_hi, ALU.subtract))
                    dve.wait_ge(bias_done, 1)
                    step_no_wait(nc.vector.tensor_tensor(attn_bias, ps8[7][:, 0:D], bo_b, ALU.add))
                    assert n_step[0] == A_DONE, n_step[0]
                if (p, s) in NORM_AT:
                    dve.wait_ge(a_rstd, 2)
                    for n in NORM_AT[p, s]:
                        for t in range(n * QT, (n + 1) * QT):
                            last = nc.vector.tensor_scalar(xn[:, t, :], xn[:, t, :], stat[:, 0, t:t + 1],
                                                           stat[:, 1, t:t + 1], ALU.subtract, ALU.mult)
                        last.then_inc(a_norm, 1)
                if (p, s) in TURN_AT:
                    for n in TURN_AT[p, s]:
                        lo_block(n)

            lo_block(0)

            def route(m, r, k):
                counted = [ROUTE_AT.get(k, 0)]

                def own(ins):
                    ins.then_inc(route_step, 1)
                    counted[0] += 1

                def settled():
                    dve.wait_ge(route_step, m * ROUTE_STEPS + counted[0])

                def then(ins):
                    own(ins)
                    settled()

                def all_tiles(row):
                    return row.unsqueeze(1).broadcast_to([P, QT, row.shape[1]])

                if k == 1:
                    if isinstance(m, int) and m == 0:
                        dve.wait_ge(scores_t, 4 * LAST)
                        dve.wait_ge(y_added, HP)
                    at = slice(m * QT, (m + 1) * QT) if isinstance(m, int) else bass.ds(m * QT, QT)
                    then(nc.vector.tensor_tensor(ya, xn[:, at, :], all_tiles(attn_bias), ALU.add))
                if k in (2, 7):
                    for t in range(QT):
                        own(nc.vector.bn_stats(bn[:, t, :], (ya if k == 2 else x2[r])[:, t, :]))
                    settled()
                if k in (3, 8):
                    for t in range(QT):
                        own(nc.vector.bn_aggr(mean_var[:, t, :], bn[:, t, :]))
                    settled()
                    eps = POST_EPS if k == 3 else LN_EPS
                    nc.vector.tensor_scalar(veps, mean_var[:, :, 1], eps, None, ALU.add).then_inc(c_var, 1)
                if k == 4:
                    for t in range(QT):
                        own(nc.vector.scalar_tensor_tensor(out=ya[:, t, :], in0=ya[:, t, :], scalar=mean_var[:, t, 0:1],
                                                           in1=gamma_b, op0=ALU.subtract, op1=ALU.mult))
                if k == 6:
                    settled()
                    dve.wait_ge(rstd_done, m * 2 + 1)
                    dve.wait_ge(xbeta, m + 1)
                    wait(dve, out_sent, (m - 1) * 16)
                    for t in range(QT):
                        own(nc.vector.scalar_tensor_tensor(out=x2[r][:, t, :], in0=ya[:, t, :], scalar=rstd[:, t:t + 1],
                                                           in1=xin[r][:, t, :], op0=ALU.mult, op1=ALU.add))
                    settled()
                if k == 9:
                    dve.wait_ge(rstd_done, m * 2 + 2)
                    wait(dve, tr_c, m)
                    for t in range(QT):
                        last = nc.vector.tensor_scalar(xf[:, t, :], x2[r][:, t, :], mean_var[:, t, 0:1],
                                                       rstd[:, t:t + 1], ALU.subtract, ALU.mult)
                    last.then_inc(xf_done, 1)
                if k == 12:
                    dve.wait_ge(tr_c_hi, m + 1)
                    nc.vector.tensor_tensor(fT_lo[r], bank_c(m), fT_hi[r], ALU.subtract).then_inc(tr_c_lo, 1)
                g8 = sfc.rearrange("p t (g e) -> p (t g) e", g=G)
                n4, n2, n1 = QT * G * 4, QT * G * 2, QT * G
                hi4, lo4 = (work1[:, i * n4:(i + 1) * n4].rearrange("p (n e) -> p n e", e=4) for i in range(2))
                hi2, mid2, lo2, sec2 = (work2[:, i * n2:(i + 1) * n2].rearrange("p (n e) -> p n e", e=2) for i in range(4))
                hi1, mid1, lo1, sec1, gsum, rank = (work1[:, i * n1:(i + 1) * n1] for i in range(6))
                if k == 16:
                    dve.wait_ge(sfc_done, m + 1)
                    own(nc.vector.tensor_tensor(hi4, g8[:, :, 0:4], g8[:, :, 4:8], ALU.max))
                    own(nc.vector.tensor_tensor(lo4, g8[:, :, 0:4], g8[:, :, 4:8], ALU.min))
                if k == 17:
                    settled()
                    own(nc.vector.tensor_tensor(hi2, hi4[:, :, 0:2], hi4[:, :, 2:4], ALU.max))
                    own(nc.vector.tensor_tensor(mid2, hi4[:, :, 0:2], hi4[:, :, 2:4], ALU.min))
                    then(nc.vector.tensor_tensor(lo2, lo4[:, :, 0:2], lo4[:, :, 2:4], ALU.max))
                    own(nc.vector.tensor_tensor(sec2, mid2, lo2, ALU.max))
                if k == 18:
                    settled()
                    own(nc.vector.tensor_tensor(hi1, hi2[:, :, 0], hi2[:, :, 1], ALU.max))
                    own(nc.vector.tensor_tensor(mid1, hi2[:, :, 0], hi2[:, :, 1], ALU.min))
                    own(nc.vector.tensor_tensor(lo1, sec2[:, :, 0], sec2[:, :, 1], ALU.max))
                if k == 19:
                    settled()
                    then(nc.vector.tensor_tensor(sec1, mid1, lo1, ALU.max))
                    own(nc.vector.tensor_tensor(gsum, hi1, sec1, ALU.add))
                mine = gsum.rearrange("p (t g) -> p t g", t=QT).unsqueeze(3).broadcast_to([P, QT, G, G])
                other = gsum.rearrange("p (t g) -> p t g", t=QT).unsqueeze(2).broadcast_to([P, QT, G, G])
                pairs3, pairs4 = (w.rearrange("p (t g h) -> p t g h", t=QT, g=G) for w in (work3, work4))
                taken, masked = (w.rearrange("p (t e) -> p t e", t=QT) for w in (work3, work4))
                if k == 20:
                    settled()
                    own(nc.vector.tensor_tensor(pairs4, other, mine, ALU.is_gt))
                    own(nc.vector.tensor_tensor(pairs3, other, mine, ALU.is_ge))
                if k == 21:
                    settled()
                    if isinstance(m, int) and m == 0:
                        dve.wait_ge(tri_done, 2)
                    then(nc.vector.tensor_tensor(taken, taken, all_tiles(tri), ALU.mult))
                    own(nc.vector.tensor_tensor(work3, work3, work4, ALU.max))
                if k == 22:
                    settled()
                    then(nc.vector.tensor_reduce(rank, work3.rearrange("p (n h) -> p n h", h=G), AX.X, ALU.add))
                    own(nc.vector.tensor_scalar(rank, rank, float(TOPG) - 0.5, None, ALU.is_lt))
                if k == 23:
                    settled()
                    then(nc.vector.tensor_tensor(work4.rearrange("p (n e) -> p n e", e=EG), g8,
                                                 rank.unsqueeze(2).broadcast_to([P, QT * G, EG]), ALU.mult))
                best = work2[:, 0:QT * TOPK].rearrange("p (t k) -> p t k", t=QT)
                if k == 24:
                    for t in range(QT):
                        own(nc.vector.max(best[:, t, :], masked[:, t, :]))
                    settled()
                if k == 25:
                    for t in range(QT):
                        own(nc.vector.match_replace(taken[:, t, :], best[:, t, :], masked[:, t, :], -3.0e38))
                    settled()
                if k == 26:
                    then(nc.vector.tensor_scalar(work3, work3, -2.0e38, None, ALU.is_lt))
                    own(nc.vector.tensor_tensor(sfc, scores, taken, ALU.mult))
                if k == 27:
                    settled()
                    then(nc.vector.tensor_reduce(total, sfc, AX.X, ALU.add))
                    then(nc.vector.tensor_scalar(total, total, 1e-20, 1 / ROUTE_SCALE, ALU.add, ALU.mult))
                    own(nc.vector.reciprocal(share, total))
                if k == 28:
                    settled()
                    nc.vector.tensor_tensor(sfc, sfc, share.unsqueeze(2).broadcast_to([P, QT, E]), ALU.mult).then_inc(coef, 1)
                assert counted[0] == ROUTE_AT.get(k, 0) + ROUTE_COUNT.get(k, 0), k

            def run(p, u, batch):
                t = p + 3

                def row_max(s, h):
                    pair, q, up = p + 1 + (s + 2) // 4, (s + 2) % 4, u + 1 + (s + 2) // 4
                    if not valid(pair):
                        return
                    dve.wait_ge(max_scores, 8 * pair + 2 * q + h + 1)
                    if q == 0 and h == 0:
                        wait(dve, negmax_done, pair - 1)
                    nc.vector.tensor_reduce(rmax[:, up % 2, q, h:h + 1], ps_max, AX.X, ALU.max).then_inc(max_done, 1)
                    if q == 3 and h == 1:
                        dve.wait_ge(max_done, 8 * pair + 8)
                        wait(dve, maxrow_ps, pair - 1)
                        nc.vector.tensor_scalar(negmax[:, up % 2, :, :], rmax[:, up % 2, :, :], -1.0 / ROW_SCALE,
                                                EXP_SHIFT / ROW_SCALE, ALU.mult, ALU.add).then_inc(negmax_done, 1)

                for s in range(4):
                    if s == 0 and valid(p, -3):
                        _, b = batch_of(u, batch, -3)
                        dve.wait_ge(y_ps, p - 3 + 1)
                        wait(dve, y_added, p - 3)
                        dst = xn[:, bass.ds(b * QT, QT), :] if not isinstance(b, int) else xn[:, b * QT:b * QT + QT, :]
                        nc.vector.tensor_tensor(dst, ps_turn.rearrange("p (t d) -> p t d", t=QT), dst,
                                                ALU.add).then_inc(y_added, 1)
                    row_max(s, 0)
                    if valid(p, -1):
                        dve.wait_ge(ctx_ps, 4 * (p - 1) + s + 1)
                        wait(dve, ctx_done, 4 * (p - 1) + s - 1)
                        nc.vector.reciprocal(rden[:, s % 2, :], ps_ctx[:, K:K + P + 1:P]).then_inc(rden_done, 1)
                    if s == 3 and (not isinstance(p, int) or -2 <= p - u % 2 < PAIRS):
                        v, vb = batch_of(u - u % 2, batch, 2)
                        tile, half = vb * (HP // 2) + v // 2, vb * (HP // 4) + v // 4
                        dst = slice(tile, tile + 1) if isinstance(tile, int) else bass.ds(tile, 1)
                        raw = w_raw[:, v // 2 % 2:v // 2 % 2 + 1, :, :]
                        if u % 2 == 0:
                            dve.wait_ge(w_in[v // 2 % 2], (half + 1) * 48)
                            nc.vector.tensor_scalar(w_hi[:, dst, :, :], raw, 1.0, None, ALU.mult).then_inc(w_hi_done, 1)
                        else:
                            dve.wait_ge(w_hi_done, tile + 1)
                            nc.vector.tensor_tensor(w_lo[:, dst, :, :], raw, w_hi[:, dst, :, :],
                                                    ALU.subtract).then_inc(w_split, 1)
                    if s == 1 and valid(p, -2):
                        dve.wait_ge(ctx_hi, p - 2 + 1)
                        nc.vector.tensor_tensor(ctxT_lo[:, u % 2, :], ps_turn, ctxT_hi[:, u % 2, :],
                                                ALU.subtract).then_inc(ctx_lo, 1)
                    row_max(s, 1)
                    if s < 2 and valid(t):
                        n = batch_of(u, batch, 3)[0]
                        dve.wait_ge(qk_hi, 2 * t + s + 1)
                        nc.vector.scalar_tensor_tensor(out=flat[:, (u + 3) % 2, (ZQL, ZKL)[s], :], in0=ps_proj,
                                                       scalar=(bq8, bk_c)[s][:, n:n + 1],
                                                       in1=flat[:, (u + 3) % 2, (ZQH, ZKH)[s], :],
                                                       op0=ALU.add, op1=ALU.subtract).then_inc(qk_lo, 1)
                    if s == 2 and valid(p):
                        dve.wait_ge(v_hi_done, p + 1)
                        nc.vector.tensor_tensor(v_lo[:, u % 2, :, :, :],
                                                ps_proj.rearrange("p (t h c) -> p t h c", t=QT, h=2),
                                                v_hi[:, u % 2, :, :, 0:K], ALU.subtract).then_inc(v_lo_done, 1)
                    if isinstance(p, int) and p < 0:
                        rest_of_a(p, s)
                    for k in block_0_at(p, s):
                        route(0, 0, k)

            steps(run, dve)

            def tile(n, r, k):
                if k >= TILES:
                    n, r, k = n + 1, 1 - r, k - TILES
                t, i = n * TILES + k, r * TILES + k
                if k > 0:
                    dve.wait_ge(coef_in[(k - 1) % 4], n * (EP // 4 * 16) + ((k - 1) // 4 + 1) * 16)
                dve.wait_ge(silu_done, t + 1)
                dve.wait_ge(u_ps, t + 1)
                if k > 0:
                    nc.vector.tensor_tensor(prod[:, i % 2, :], silu_g[:, i % 3, :], ps8[3 + i % 3],
                                            ALU.mult).then_inc(prod_done, 1)
                    dve.wait_ge(prod_done, t + 1)
                wait(dve, hid_lo_done, t - 5)
                if k > 0:
                    nc.vector.tensor_tensor(hid[:, i % 6, :], prod[:, i % 2, :], coef_b[:, (k - 1) % 4, :],
                                            ALU.mult).then_inc(hid_done, 1)
                else:
                    nc.vector.tensor_tensor(hid[:, i % 6, :], silu_g[:, i % 3, :], ps8[3 + i % 3],
                                            ALU.mult).then_inc(hid_done, 1)
                    dve.wait_ge(hid_done, t + 1)
                    nc.vector.tensor_copy(prod[:, i % 2, 0:2], hid[:, i % 6, 0:2]).then_inc(prod_done, 1)

            def add_sum(n, r):
                dve.wait_ge(y_back, n + 1)
                nc.vector.tensor_tensor(x2[r], ps8[7].rearrange("p (t d) -> p t d", t=QT), x2[r],
                                        ALU.add).then_inc(out_ready, 1)

            def run_block(n, r, last):
                for k in range(1, TILES if last else TILES + 1):
                    tile(n, r, k)
                    if k == 3 and (not isinstance(n, int) or n > 0):
                        add_sum(n - 1, 1 - r)
                    if not last:
                        route(n + 1, 1 - r, k)

            dve.wait_ge(y_added, PAIRS)
            tile(0, 0, 0)
            blocks(dve, run_block)
            add_sum(B - 1, (B - 1) % 2)

        @block.tensor
        def _(pe):
            def mm(out_, lhsT, rhs, start, stop):
                return nc.tensor.matmul(out_, lhsT, rhs, start=start, stop=stop, skip_group_check=True)

            def product(out_, a_hi, a_lo, b_hi, b_lo, start=True, stop=True):
                mm(out_, a_hi, b_hi, start, False)
                mm(out_, a_hi, b_lo, False, False)
                return mm(out_, a_lo, b_hi, False, stop)

            def transposes(n):
                if n >= NORM_POOL:
                    pe.wait_ge(a_norm_pool, n - NORM_POOL + 1)
                elif n >= 1:
                    pe.wait_ge(a_norm, n)
                if n >= 4:
                    pe.wait_ge(tr_a_lo, n - 3)
                for t in range(QT):
                    last = nc.tensor.transpose(ps8[n % 4][:, t * P:(t + 1) * P], xn[:, n * QT + t, :], ident)
                last.then_inc(tr_a, 1)

            def rest_of_a(p, s):
                if (p, s) == (-2, 1):
                    pe.wait_ge(in_rest, 8 * 16)
                    nc.tensor.transpose(ps8[5][:, 0:E], router_raw[0:E, :], ident[0:E, 0:E]).then_inc(router_t, 1)
                if (p, s) == (-2, 3):
                    pe.wait_ge(bv_spread, HP)
                    for n in range(HP):
                        last = mm(ps8[7][:, 0:D], bv_rows[:, n, :], raw_o[:, n * D:(n + 1) * D], n == 0, n == HP - 1)
                    last.then_inc(bias_done, 1)
                if (p, s) in TURN_AT:
                    for n in TURN_AT[p, s]:
                        transposes(n)
                if (p, s) == (-1, 1):
                    pe.wait_ge(dve_step, A_DONE)

            pe.wait_ge(pool_const, 2)
            pe.wait_ge(dve_step, XN_READY)
            transposes(0)
            pe.wait_ge(dve_step, QK_READY)
            pe.wait_ge(tr_a_lo, 1)

            def tokens(pair, u, off=0, n=S):
                if isinstance(pair, int):
                    at = pair // HP * S + off
                    return xT_hi[:, at:at + n], xT_lo[:, at:at + n]
                return tuple(x_[:, off:off + n] for x_ in xT_of[u % HP // (HP // 2)])

            def route(m, r, k):
                if k == 8:
                    pe.wait_ge(xf_done, m + 1)
                    if isinstance(m, int) and m == 0:
                        pe.wait_ge(max_done, 8 * PAIRS)
                    for t in range(QT):
                        last = nc.tensor.transpose(bank_c(m)[:, t * P:(t + 1) * P], xf[:, t, :], ident)
                    last.then_inc(tr_c, 1)
                if k == 11:
                    pe.wait_ge(tr_c_lo, m + 1)
                    for t in range(QT):
                        ts_ = slice(t * P, (t + 1) * P)
                        last = product(bank_c(m)[:, t * E:(t + 1) * E], fT_hi[r][:, ts_], fT_lo[r][:, ts_], router_hi, router_lo)
                    last.then_inc(logits, 1)
                if k == 27:
                    if isinstance(m, int) and m == 0:
                        pe.wait_ge(coef, 1)
                    for t in range(QT):
                        last = nc.tensor.transpose(bank_c(m)[0:E, t * P:(t + 1) * P], sfc[:, t, :], ident)
                    last.then_inc(coef_t, 1)

            def gate_up(n, r, k):
                if k >= TILES:
                    n, r, k = n + 1, 1 - r, k - TILES
                t, i = n * TILES + k, r * TILES + k
                wait(pe, silu_done, t - 2)
                product(ps8[i % 3], w_hi[:, k, 0, :], w_lo[:, k, 0, :], fT_hi[r], fT_lo[r]).then_inc(g_ps, 1)
                wait(pe, prod_done, t - 2)
                product(ps8[3 + i % 3], w_hi[:, k, 1, :], w_lo[:, k, 1, :], fT_hi[r], fT_lo[r]).then_inc(u_ps, 1)

            def run(p, u, batch):
                t = p + 3

                def query_tile(s, h):
                    pair, q, up = p + 1 + (s + 2) // 4, (s + 2) % 4, u + 1 + (s + 2) // 4
                    if not valid(pair):
                        return
                    if q == 0 and h == 0:
                        half = (p + 2) // 2 if isinstance(p, int) else batch * (HP // 2) + (u + 2) // 2
                        pe.wait_ge(stacked[up % 2], 96 * (half + 1))
                    wait(pe, max_done, 8 * pair + 2 * q + h)
                    st = stack[:, up % 4, h, :, :]
                    mm(ps_max, st[:, Q1, q * P:(q + 1) * P], st[:, K1, :], True, True).then_inc(max_scores, 1)

                for s in range(4):
                    if valid(p):
                        if s == 0:
                            pe.wait_ge(maxrow, p + 1)
                        if isinstance(p, int) and p == 0 and s == 0:
                            pe.wait_ge(tr_a_lo, B)
                        wait(pe, exp_done, 4 * p + s - 1)
                        ks = slice(s * P, (s + 1) * P)
                        for h in range(2):
                            o = ps_st[s % 2][:, h * S:(h + 1) * S]
                            st = stack[:, u % 4, h, :, :]
                            mm(o, st[:, K1, ks], st[:, Q1, :], True, False)
                            last = mm(o, st[0:K + 2, K2, ks], st[0:K + 2, Q2, :], False, True)
                        last.then_inc(scores_t, 1)
                    if valid(p, -1):
                        h, q0, o = s // 2, 2 * (s % 2), (u + 1) % 2
                        wait(pe, ctx_done, 4 * (p - 1) + s)
                        if s == 0:
                            pe.wait_ge(v_lo_done, p)
                        for k in range(QT):
                            if s == 0:
                                pe.wait_ge(lo_pool, 4 * (p - 1) + k + 1)
                            for q in range(2):
                                qs = slice((q0 + q) * P, (q0 + q + 1) * P)
                                c = ps_ctx[:, q * P:q * P + K + 1]
                                mm(c, num_hi[:, o, k, h, qs, 1], v_hi[:, o, k, h, :], k == 0 and q == 0, False)
                                mm(c[:, 0:K], num_hi[:, o, k, h, qs, 1], v_lo[:, o, k, h, :], False, False)
                                last = mm(c, num_lo[:, o, k, h, qs], v_hi[:, o, k, h, :], False, k == QT - 1)
                            if k == 0:
                                query_tile(s, 0)
                        last.then_inc(ctx_ps, 1)
                    else:
                        query_tile(s, 0)
                    if s == 2 and valid(p, 1):
                        wait(pe, ctx_lo, p - 2 + 1)
                        if isinstance(p, int):
                            wait(pe, maxrow, p + 1)
                        pe.wait_ge(negmax_done, p + 1 + 1)
                        for k in range(QT):
                            last = mm(ps_turn[K:K + 2, k * P:(k + 1) * P], negmax[:, (u + 1) % 2, k, :], ident16, True, True)
                        last.then_inc(maxrow_ps, 1)
                    if s < 2 and valid(t):
                        n, b = batch_of(u, batch, 3)
                        wh, wl = ((wq_hi, wq_lo), (wk_hi, wk_lo))[s]
                        if s == 0 and not isinstance(t, int) and n % (HP // 2) == 0:
                            pe.wait_ge(x_of[n // (HP // 2)], (b + n // (HP // 2)) * 32)
                        if s == 0:
                            wait(pe, v_lo_done, p)
                            if isinstance(t, int):
                                wait(pe, qk_lo, 2 * t)
                        else:
                            pe.wait_ge(qk_lo, 2 * t + 1)
                        product(ps_proj, wh[:, n, :], wl[:, n, :], *tokens(t, u + 3)).then_inc(qk_proj, 1)
                    if s == 2 and valid(p):
                        n, _ = batch_of(u, batch, 0)
                        pe.wait_ge(qk_lo, upto(2 * t + 2, 2 * PAIRS))
                        for k in range(QT):
                            last = product(ps_proj[:, k * P:(k + 1) * P], *tokens(p, u, k * P, P),
                                           wv_hi[:, n, :], wv_lo[:, n, :])
                        last.then_inc(v_proj, 1)
                    if s == 3 and valid(p, -2):
                        n, _ = batch_of(u, batch, -2)
                        pe.wait_ge(ctx_lo, p - 2 + 1)
                        pe.wait_ge(maxrow, upto(p + 1 + 1, PAIRS))
                        for k in range(QT):
                            ks = slice(k * P, (k + 1) * P)
                            last = product(ps_turn[:, ks], ctxT_hi[:, u % 2, ks], ctxT_lo[:, u % 2, ks],
                                           wo_hi[:, n, :], wo_lo[:, n, :])
                        last.then_inc(y_ps, 1)
                    query_tile(s, 1)
                    if s == 0 and valid(p, -2):
                        wait(pe, y_added, p - 2)
                        if isinstance(p, int):
                            wait(pe, maxrow, upto(p + 1, PAIRS))
                        pe.wait_ge(ctx_done, 4 * (p - 2) + 4)
                        for k in range(QT):
                            last = nc.tensor.transpose(ps_turn[:, k * P:(k + 1) * P], ctxn[:, u % 2, k, :], ident)
                        last.then_inc(ctx_t, 1)
                    if isinstance(p, int) and p < 0:
                        rest_of_a(p, s)
                    if isinstance(p, int) and p == FIRST - 1 and s == 3:
                        pe.wait_ge(x_of[1], 32)
                    for k in block_0_at(p, s):
                        route(0, 0, k - 2)
                    if isinstance(p, int) and (p, s) == (PAIRS + 1, 1):
                        pe.wait_ge(w_split, TILES)
                        pe.wait_ge(exp_done, 4 * PAIRS)
                        gate_up(0, 0, 0)

            steps(run, pe)

            def down(n, r, k):
                if k == TILES:
                    n, r, k = n + 1, 1 - r, 0
                t, i = n * TILES + k, r * TILES + k
                pe.wait_ge(hid_lo_done, t + 1)
                if k == 0:
                    wait(pe, y_copied, n)
                product(ps8[6], w_hi[:, k, 2, :], w_lo[:, k, 2, :], hid_hi[:, i % 6, :], hid_lo[:, i % 6, :],
                        start=k == 0, stop=k == TILES - 1).then_inc(down_done, 1)

            def transpose_sum(n):
                pe.wait_ge(y_copied, n + 1)
                for k in range(QT):
                    last = nc.tensor.transpose(ps8[7][:, k * P:(k + 1) * P], ysb[:, k * P:(k + 1) * P], ident)
                last.then_inc(y_back, 1)

            def run_block(n, r, last):
                for k in range(1, TILES if last else TILES + 1):
                    if not (last and k + 4 >= TILES):
                        gate_up(n, r, k + 4)
                    if k == 27 and not last:
                        pe.wait_ge(coef, n + 2)
                    down(n, r, k)
                    if not last:
                        route(n + 1, 1 - r, k)
                transpose_sum(n)

            pe.wait_ge(coef_sb, 1)
            for k in range(1, 5):
                gate_up(0, 0, k)
            down(0, 0, 0)
            blocks(pe, run_block)


A_VAR0 = QT + 7
XN_READY = A_VAR0 + QT
QK_READY = XN_READY + 3
A_VAR1 = QK_READY + NT - QT + 7
A_DONE = A_VAR1 + 4
ACT_QK = 1 + 8 + 2
ACT_REST = ACT_QK + 3

STATS_AT = {(-3, 0): (QT, 3 * QT), (-3, 1): (3 * QT, 5 * QT), (-3, 2): (5 * QT, 6 * QT),
            (-2, 0): (6 * QT, 7 * QT), (-2, 1): (7 * QT, NT)}
NORM_AT = {(-2, 3): (1, 2), (-1, 0): (3, 4), (-1, 1): (5,)}
NORM_POOL = 6
TURN_AT = {(-1, 0): (1,), (-1, 1): (2, 3), (-1, 2): (4, 5), (-1, 3): (6, 7)}

ROUTE_COUNT = {1: 1, 2: QT, 3: QT, 4: QT, 6: QT, 7: QT, 8: QT, 16: 2, 17: 4, 18: 3, 19: 2,
               20: 2, 21: 2, 22: 2, 23: 1, 24: QT, 25: QT, 26: 2, 27: 3, 28: 0}
ROUTE_AT = {k: sum(c for j, c in ROUTE_COUNT.items() if j < k) for k in ROUTE_COUNT}
C_PARTS = 31
ROUTE_STEPS = sum(ROUTE_COUNT.values())


_INS = ["x", "Wq", "bq", "Wk", "bk", "Wv", "bv", "Wo", "bo", "gamma", "beta"]
_FFN = ["router_w", "e_bias", "Wg", "Wu", "Wd", "SWg", "SWu", "SWd"]


def kernel(**inputs):
    import numpy as np
    import concourse.bacc as bacc
    from concourse.bass_utils import run_bass_kernel_spmd

    nc = bacc.Bacc("TRN2", target_bir_lowering=False, num_devices=1)
    arrays, args = {}, []
    for name in ["L0_attn_" + n for n in _INS] + ["L0_ffn_" + n for n in _FFN]:
        a = np.ascontiguousarray(inputs[name])
        arrays[f"in_{name}"] = a
        args.append(nc.dram_tensor(f"in_{name}", a.shape, mybir.dt.from_np(a.dtype), kind="ExternalInput").ap())
    out = nc.dram_tensor("out_0", (B, S, D), F32, kind="ExternalOutput").ap()
    layer(nc, *args, out)
    result = run_bass_kernel_spmd(nc, [arrays], core_ids=[0])
    return result.results[0]["out_0"]
```
